# Optimizing a Trainium2 kernel written in Bass

```python
import numpy as np
import jax
import jax.numpy as jnp

def _softmax(x, axis=-1):
    return jax.nn.softmax(x, axis=axis)

def _gelu(x):
    return jax.nn.gelu(x, approximate=True)

def _silu(x):
    return jax.nn.silu(x)

def _sigmoid(x):
    return jax.nn.sigmoid(x)

def _layernorm(x, axis=-1, eps=1e-05):
    m = jnp.mean(x, axis=axis, keepdims=True)
    v = jnp.var(x, axis=axis, keepdims=True)
    return (x - m) / jnp.sqrt(v + eps)

def _scatter_add(tgt, idx, src, axis=0):
    return tgt.at[idx].add(src)

def _segment_sum(src, seg, n):
    return jax.ops.segment_sum(src, seg, n)
kernel_name = 'mk_conv_seq_d4_conv_nchw256_r2_3ae6a3'

def setup_inputs(seed: int=0):
    np.random.seed(seed)
    _w = jnp.asarray

    def _rec_inputs():
        import jax
        import jax.numpy as jnp
        _gk = jax.random.key(seed)
        x = -0.0001329 + 0.9999 * jax.random.normal(jax.random.fold_in(_gk, 1), (4, 128, 96, 96), jnp.float32)
        return x
    x = _rec_inputs()

    def _L0_conv_setup():
        import jax, jax.numpy as jnp
        import numpy as np
        EPS = 1e-05

        def _bn(x, gamma, beta, mean, var):
            scale = gamma * jax.lax.rsqrt(var + EPS)
            return (x - mean[:, None, None]) * scale[:, None, None] + beta[:, None, None]

        def _prelu(x, alpha):
            a = alpha[0]
            return jnp.where(x >= 0, x, a * x)

        def _up2_nearest(x):
            return jnp.repeat(jnp.repeat(x, 2, axis=2), 2, axis=3)
        key = jax.random.key(seed)
        ks = jax.random.split(key, 12)
        B, C, H, W = (8, 128, 96, 96)
        x = jax.random.normal(ks[0], (B, C, H, W), dtype=jnp.float32)
        mag_w = jax.random.normal(ks[1], (C, C), dtype=jnp.float32) * (1.0 / np.sqrt(C))
        mag_b = jax.random.normal(ks[2], (C,), dtype=jnp.float32) * 0.01
        phase_w = jax.random.normal(ks[3], (2 * C, 2 * C), dtype=jnp.float32) * (1.0 / np.sqrt(2 * C))
        phase_b = jax.random.normal(ks[4], (2 * C,), dtype=jnp.float32) * 0.01
        mag_gamma = jnp.ones((C,), jnp.float32)
        mag_beta = jnp.zeros((C,), jnp.float32)
        mag_mean = jax.random.normal(ks[5], (C,), dtype=jnp.float32) * 0.1
        mag_var = jax.random.uniform(ks[6], (C,), jnp.float32, 0.5, 1.5)
        phase_gamma = jnp.ones((2 * C,), jnp.float32)
        phase_beta = jnp.zeros((2 * C,), jnp.float32)
        phase_mean = jax.random.normal(ks[7], (2 * C,), dtype=jnp.float32) * 0.1
        phase_var = jax.random.uniform(ks[8], (2 * C,), jnp.float32, 0.5, 1.5)
        alpha = jnp.full((1,), 0.25, jnp.float32)
        return {'x': x, 'mag_w': mag_w, 'mag_b': mag_b, 'phase_w': phase_w, 'phase_b': phase_b, 'mag_gamma': mag_gamma, 'mag_beta': mag_beta, 'mag_mean': mag_mean, 'mag_var': mag_var, 'phase_gamma': phase_gamma, 'phase_beta': phase_beta, 'phase_mean': phase_mean, 'phase_var': phase_var, 'alpha': alpha}
    _L0_conv_all = _L0_conv_setup()
    _L0_conv_in = {k: v for k, v in _L0_conv_all.items() if k in ('mag_w', 'mag_b', 'phase_w', 'phase_b', 'mag_gamma', 'mag_beta', 'mag_mean', 'mag_var', 'phase_gamma', 'phase_beta', 'phase_mean', 'phase_var', 'alpha')}
    del _L0_conv_all

    def _L1_conv_setup():
        import jax, jax.numpy as jnp
        import numpy as np
        B, C1, C2, H, W = (4, 128, 128, 64, 64)
        Cm = int(C2 * 0.5)
        K = 4
        N = 1
        R = 8

        def conv1x1(x, w, b=None):
            y = jnp.einsum('bchw,oc->bohw', x, w)
            return y if b is None else y + b[None, :, None, None]

        def selective_scan(u, dt, A, Bs, Cs, Dsk):
            a = jnp.exp(dt[..., None] * A[None, :, :, None, :])
            b = (dt * u)[..., None] * Bs.transpose(0, 1, 3, 2)[:, :, None]

            def comb(e1, e2):
                a1, b1 = e1
                a2, b2 = e2
                return (a2 * a1, a2 * b1 + b2)
            _, h = jax.lax.associative_scan(comb, (a, b), axis=3)
            return jnp.einsum('bkdln,bknl->bkdl', h, Cs) + Dsk[None, :, :, None] * u

        def ss2d(xin, in_proj_w, conv_w, conv_b, x_proj_w, dt_w, dt_b, A_logs, Ds, ln_g, ln_b, out_proj_w):
            Bb, _, Hh, Ww = xin.shape
            L = Hh * Ww
            xz = conv1x1(xin, in_proj_w)
            xc, z = (xz[:, :Cm], xz[:, Cm:])
            z = jax.nn.silu(z)
            xc = jax.lax.conv_general_dilated(xc, conv_w, (1, 1), 'SAME', feature_group_count=Cm, dimension_numbers=('NCHW', 'OIHW', 'NCHW')) + conv_b[None, :, None, None]
            xc = jax.nn.silu(xc)
            xh = xc.reshape(Bb, Cm, L)
            xw = xc.transpose(0, 1, 3, 2).reshape(Bb, Cm, L)
            xs = jnp.stack([xh, xw, xh[..., ::-1], xw[..., ::-1]], axis=1)
            x_dbl = jnp.einsum('bkdl,kcd->bkcl', xs, x_proj_w)
            dts, Bs, Cs = jnp.split(x_dbl, [R, R + N], axis=2)
            dts = jnp.einsum('bkrl,kdr->bkdl', dts, dt_w)
            dt = jax.nn.softplus(dts + dt_b[None, :, :, None])
            A = -jnp.exp(A_logs).reshape(K, Cm, N)
            ys = selective_scan(xs, dt, A, Bs, Cs, Ds.reshape(K, Cm))
            y02 = ys[:, 0] + ys[:, 2, :, ::-1]
            y13 = ys[:, 1] + ys[:, 3, :, ::-1]
            y = y02.reshape(Bb, Cm, Hh, Ww) + y13.reshape(Bb, Cm, Ww, Hh).transpose(0, 1, 3, 2)
            mu = y.mean(axis=1, keepdims=True)
            var = y.var(axis=1, keepdims=True)
            y = (y - mu) / jnp.sqrt(var + 1e-05) * ln_g[None, :, None, None] + ln_b[None, :, None, None]
            y = y * z
            return conv1x1(y, out_proj_w)
        key = jax.random.key(seed)
        ks = jax.random.split(key, 16)
        rn = lambda k, shp, s=0.1: jax.random.normal(k, shp, jnp.float32) * s
        return {'x': jax.random.normal(ks[0], (B, C1, H, W), jnp.float32), 'cv1_w': rn(ks[1], (Cm, C1)), 'cv1_b': rn(ks[2], (Cm,)), 'scale_w': jnp.full((1, Cm, 1, 1), 0.1, jnp.float32), 'in_proj_w': rn(ks[3], (2 * Cm, Cm)), 'conv_w': rn(ks[4], (Cm, 1, 3, 3)), 'conv_b': rn(ks[5], (Cm,)), 'x_proj_w': rn(ks[6], (K, R + 2 * N, Cm)), 'dt_w': rn(ks[7], (K, Cm, R)), 'dt_b': rn(ks[8], (K, Cm)), 'A_logs': rn(ks[9], (K * Cm, N)), 'Ds': jnp.ones((K * Cm,), jnp.float32), 'ln_g': jnp.ones((Cm,), jnp.float32), 'ln_b': jnp.zeros((Cm,), jnp.float32), 'out_proj_w': rn(ks[10], (Cm, Cm)), 'cv2_w': rn(ks[11], (C2, Cm)), 'cv2_b': rn(ks[12], (C2,))}
    _L1_conv_all = _L1_conv_setup()
    _L1_conv_in = {k: v for k, v in _L1_conv_all.items() if k in ('cv1_w', 'cv1_b', 'scale_w', 'in_proj_w', 'conv_w', 'conv_b', 'x_proj_w', 'dt_w', 'dt_b', 'A_logs', 'Ds', 'ln_g', 'ln_b', 'out_proj_w', 'cv2_w', 'cv2_b')}
    del _L1_conv_all

    def _L2_conv_setup():
        import jax, jax.numpy as jnp
        import numpy as np
        B, DIM, H, W = (8, 128, 32, 32)
        HEADS = 8
        MLP_RATIO = 4.0

        def _dwconv(x, w, b):
            C = x.shape[1]
            y = jax.lax.conv_general_dilated(x, w, window_strides=(1, 1), padding='SAME', dimension_numbers=('NCHW', 'OIHW', 'NCHW'), feature_group_count=C)
            return y + b[None, :, None, None]

        def _ln(x, g, b):
            m = x.mean(-1, keepdims=True)
            v = ((x - m) ** 2).mean(-1, keepdims=True)
            return (x - m) * jax.lax.rsqrt(v + 1e-05) * g + b

        def _rope(x):
            bb, Hh, Ww, c = x.shape
            k_max = c // 4
            theta = 1.0 / 10000.0 ** (jnp.arange(k_max, dtype=x.dtype) / k_max)
            ah = jnp.arange(Hh, dtype=x.dtype)[:, None] * theta
            aw = jnp.arange(Ww, dtype=x.dtype)[:, None] * theta
            ang = jnp.concatenate([jnp.broadcast_to(ah[:, None, :], (Hh, Ww, k_max)), jnp.broadcast_to(aw[None, :, :], (Hh, Ww, k_max))], -1)
            cos, sin = (jnp.cos(ang), jnp.sin(ang))
            xr = x.reshape(bb, Hh, Ww, c // 2, 2)
            re, im = (xr[..., 0], xr[..., 1])
            out = jnp.stack([re * cos - im * sin, re * sin + im * cos], -1)
            return out.reshape(bb, Hh, Ww, c)

        def _attn(x, Hh, Ww, qk_w, qk_b, lepe_w, lepe_b):
            b, n, c = x.shape
            h = HEADS
            d = c // h
            qk = x @ qk_w + qk_b
            q = jax.nn.elu(qk[..., :c]) + 1.0
            k = jax.nn.elu(qk[..., c:]) + 1.0
            v = x
            qr = _rope(q.reshape(b, Hh, Ww, c)).reshape(b, n, h, d)
            kr = _rope(k.reshape(b, Hh, Ww, c)).reshape(b, n, h, d)
            qh = q.reshape(b, n, h, d)
            kh = k.reshape(b, n, h, d)
            vh = v.reshape(b, n, h, d)
            kmean = kh.mean(axis=1)
            z = 1.0 / (jnp.einsum('bnhd,bhd->bnh', qh, kmean) + 1e-06)
            kv = jnp.einsum('bnhd,bnhe->bhde', kr, vh) * (1.0 / n)
            out = jnp.einsum('bnhd,bhde->bnhe', qr, kv) * z[..., None]
            out = out.reshape(b, n, c)
            v2d = v.reshape(b, Hh, Ww, c).transpose(0, 3, 1, 2)
            lepe = _dwconv(v2d, lepe_w, lepe_b).transpose(0, 2, 3, 1).reshape(b, n, c)
            return out + lepe

        def _forward(x, cpe1_w, cpe1_b, n1_g, n1_b, inproj_w, inproj_b, actproj_w, actproj_b, dwc_w, dwc_b, qk_w, qk_b, lepe_w, lepe_b, outproj_w, outproj_b, cpe2_w, cpe2_b, n2_g, n2_b, fc1_w, fc1_b, fc2_w, fc2_b):
            Bb, C, Hh, Ww = x.shape
            n = Hh * Ww

            def tok2img(t):
                return t.reshape(Bb, Hh, Ww, C).transpose(0, 3, 1, 2)

            def img2tok(i):
                return i.transpose(0, 2, 3, 1).reshape(Bb, n, C)
            t = img2tok(x)
            t = t + img2tok(_dwconv(tok2img(t), cpe1_w, cpe1_b))
            shortcut = t
            tn = _ln(t, n1_g, n1_b)
            act_res = jax.nn.silu(tn @ actproj_w + actproj_b)
            ti = tn @ inproj_w + inproj_b
            ti = jax.nn.silu(img2tok(_dwconv(tok2img(ti), dwc_w, dwc_b)))
            ta = _attn(ti, Hh, Ww, qk_w, qk_b, lepe_w, lepe_b)
            t = shortcut + ta * act_res @ outproj_w + outproj_b
            t = t + img2tok(_dwconv(tok2img(t), cpe2_w, cpe2_b))
            tn2 = _ln(t, n2_g, n2_b)
            mlp = jax.nn.gelu(tn2 @ fc1_w + fc1_b, approximate=False) @ fc2_w + fc2_b
            t = t + mlp
            return tok2img(t)
        key = jax.random.key(seed)
        ks = jax.random.split(key, 12)
        C = DIM
        Hd = int(C * MLP_RATIO)
        s = 0.02
        f32 = jnp.float32
        return {'x': jax.random.normal(ks[0], (B, C, H, W), f32), 'cpe1_w': jax.random.normal(ks[1], (C, 1, 3, 3), f32) * s, 'cpe1_b': jnp.zeros((C,), f32), 'n1_g': jnp.ones((C,), f32), 'n1_b': jnp.zeros((C,), f32), 'inproj_w': jax.random.normal(ks[2], (C, C), f32) * s, 'inproj_b': jnp.zeros((C,), f32), 'actproj_w': jax.random.normal(ks[3], (C, C), f32) * s, 'actproj_b': jnp.zeros((C,), f32), 'dwc_w': jax.random.normal(ks[4], (C, 1, 3, 3), f32) * s, 'dwc_b': jnp.zeros((C,), f32), 'qk_w': jax.random.normal(ks[5], (C, 2 * C), f32) * s, 'qk_b': jnp.zeros((2 * C,), f32), 'lepe_w': jax.random.normal(ks[6], (C, 1, 3, 3), f32) * s, 'lepe_b': jnp.zeros((C,), f32), 'outproj_w': jax.random.normal(ks[7], (C, C), f32) * s, 'outproj_b': jnp.zeros((C,), f32), 'cpe2_w': jax.random.normal(ks[8], (C, 1, 3, 3), f32) * s, 'cpe2_b': jnp.zeros((C,), f32), 'n2_g': jnp.ones((C,), f32), 'n2_b': jnp.zeros((C,), f32), 'fc1_w': jax.random.normal(ks[9], (C, Hd), f32) * s, 'fc1_b': jnp.zeros((Hd,), f32), 'fc2_w': jax.random.normal(ks[10], (Hd, C), f32) * s, 'fc2_b': jnp.zeros((C,), f32)}
    _L2_conv_all = _L2_conv_setup()
    _L2_conv_in = {k: v for k, v in _L2_conv_all.items() if k in ('cpe1_w', 'cpe1_b', 'n1_g', 'n1_b', 'inproj_w', 'inproj_b', 'actproj_w', 'actproj_b', 'dwc_w', 'dwc_b', 'qk_w', 'qk_b', 'lepe_w', 'lepe_b', 'outproj_w', 'outproj_b', 'cpe2_w', 'cpe2_b', 'n2_g', 'n2_b', 'fc1_w', 'fc1_b', 'fc2_w', 'fc2_b')}
    del _L2_conv_all

    def _L3_conv_setup():
        import jax, jax.numpy as jnp
        import numpy as np
        STRIDE = 1
        PADDING = 1

        def _binary_activation(x):
            out_forward = jnp.sign(x)
            m1 = (x < -1).astype(x.dtype)
            m2 = (x < 0).astype(x.dtype)
            m3 = (x < 1).astype(x.dtype)
            out1 = -1.0 * m1 + (x * x + 2.0 * x) * (1.0 - m1)
            out2 = out1 * m2 + (-x * x + 2.0 * x) * (1.0 - m2)
            out3 = out2 * m3 + 1.0 * (1.0 - m3)
            return jax.lax.stop_gradient(out_forward) - jax.lax.stop_gradient(out3) + out3

        def _binary_weights(w):
            scaling = jax.lax.stop_gradient(jnp.mean(jnp.abs(w), axis=(1, 2, 3), keepdims=True))
            bw_no_grad = scaling * jnp.sign(w)
            clipped = jnp.clip(w, -1.0, 1.0)
            return jax.lax.stop_gradient(bw_no_grad) - jax.lax.stop_gradient(clipped) + clipped
        key = jax.random.key(seed)
        kx, kw = jax.random.split(key)
        x = jax.random.normal(kx, (32, 128, 56, 56), dtype=jnp.float32)
        weight = jax.random.uniform(kw, (128, 128, 3, 3), dtype=jnp.float32) * 0.001
        return {'x': x, 'weight': weight}
    _L3_conv_all = _L3_conv_setup()
    _L3_conv_in = {k: v for k, v in _L3_conv_all.items() if k in ('weight',)}
    del _L3_conv_all
    return {'x': x, 'L0_conv_mag_w': _L0_conv_in['mag_w'], 'L0_conv_mag_b': _L0_conv_in['mag_b'], 'L0_conv_phase_w': _L0_conv_in['phase_w'], 'L0_conv_phase_b': _L0_conv_in['phase_b'], 'L0_conv_mag_gamma': _L0_conv_in['mag_gamma'], 'L0_conv_mag_beta': _L0_conv_in['mag_beta'], 'L0_conv_mag_mean': _L0_conv_in['mag_mean'], 'L0_conv_mag_var': _L0_conv_in['mag_var'], 'L0_conv_phase_gamma': _L0_conv_in['phase_gamma'], 'L0_conv_phase_beta': _L0_conv_in['phase_beta'], 'L0_conv_phase_mean': _L0_conv_in['phase_mean'], 'L0_conv_phase_var': _L0_conv_in['phase_var'], 'L0_conv_alpha': _L0_conv_in['alpha'], 'L1_conv_cv1_w': _L1_conv_in['cv1_w'], 'L1_conv_cv1_b': _L1_conv_in['cv1_b'], 'L1_conv_scale_w': _L1_conv_in['scale_w'], 'L1_conv_in_proj_w': _L1_conv_in['in_proj_w'], 'L1_conv_conv_w': _L1_conv_in['conv_w'], 'L1_conv_conv_b': _L1_conv_in['conv_b'], 'L1_conv_x_proj_w': _L1_conv_in['x_proj_w'], 'L1_conv_dt_w': _L1_conv_in['dt_w'], 'L1_conv_dt_b': _L1_conv_in['dt_b'], 'L1_conv_A_logs': _L1_conv_in['A_logs'], 'L1_conv_Ds': _L1_conv_in['Ds'], 'L1_conv_ln_g': _L1_conv_in['ln_g'], 'L1_conv_ln_b': _L1_conv_in['ln_b'], 'L1_conv_out_proj_w': _L1_conv_in['out_proj_w'], 'L1_conv_cv2_w': _L1_conv_in['cv2_w'], 'L1_conv_cv2_b': _L1_conv_in['cv2_b'], 'L2_conv_cpe1_w': _L2_conv_in['cpe1_w'], 'L2_conv_cpe1_b': _L2_conv_in['cpe1_b'], 'L2_conv_n1_g': _L2_conv_in['n1_g'], 'L2_conv_n1_b': _L2_conv_in['n1_b'], 'L2_conv_inproj_w': _L2_conv_in['inproj_w'], 'L2_conv_inproj_b': _L2_conv_in['inproj_b'], 'L2_conv_actproj_w': _L2_conv_in['actproj_w'], 'L2_conv_actproj_b': _L2_conv_in['actproj_b'], 'L2_conv_dwc_w': _L2_conv_in['dwc_w'], 'L2_conv_dwc_b': _L2_conv_in['dwc_b'], 'L2_conv_qk_w': _L2_conv_in['qk_w'], 'L2_conv_qk_b': _L2_conv_in['qk_b'], 'L2_conv_lepe_w': _L2_conv_in['lepe_w'], 'L2_conv_lepe_b': _L2_conv_in['lepe_b'], 'L2_conv_outproj_w': _L2_conv_in['outproj_w'], 'L2_conv_outproj_b': _L2_conv_in['outproj_b'], 'L2_conv_cpe2_w': _L2_conv_in['cpe2_w'], 'L2_conv_cpe2_b': _L2_conv_in['cpe2_b'], 'L2_conv_n2_g': _L2_conv_in['n2_g'], 'L2_conv_n2_b': _L2_conv_in['n2_b'], 'L2_conv_fc1_w': _L2_conv_in['fc1_w'], 'L2_conv_fc1_b': _L2_conv_in['fc1_b'], 'L2_conv_fc2_w': _L2_conv_in['fc2_w'], 'L2_conv_fc2_b': _L2_conv_in['fc2_b'], 'L3_conv_weight': _L3_conv_in['weight']}

def reference(x, L0_conv_mag_w, L0_conv_mag_b, L0_conv_phase_w, L0_conv_phase_b, L0_conv_mag_gamma, L0_conv_mag_beta, L0_conv_mag_mean, L0_conv_mag_var, L0_conv_phase_gamma, L0_conv_phase_beta, L0_conv_phase_mean, L0_conv_phase_var, L0_conv_alpha, L1_conv_cv1_w, L1_conv_cv1_b, L1_conv_scale_w, L1_conv_in_proj_w, L1_conv_conv_w, L1_conv_conv_b, L1_conv_x_proj_w, L1_conv_dt_w, L1_conv_dt_b, L1_conv_A_logs, L1_conv_Ds, L1_conv_ln_g, L1_conv_ln_b, L1_conv_out_proj_w, L1_conv_cv2_w, L1_conv_cv2_b, L2_conv_cpe1_w, L2_conv_cpe1_b, L2_conv_n1_g, L2_conv_n1_b, L2_conv_inproj_w, L2_conv_inproj_b, L2_conv_actproj_w, L2_conv_actproj_b, L2_conv_dwc_w, L2_conv_dwc_b, L2_conv_qk_w, L2_conv_qk_b, L2_conv_lepe_w, L2_conv_lepe_b, L2_conv_outproj_w, L2_conv_outproj_b, L2_conv_cpe2_w, L2_conv_cpe2_b, L2_conv_n2_g, L2_conv_n2_b, L2_conv_fc1_w, L2_conv_fc1_b, L2_conv_fc2_w, L2_conv_fc2_b, L3_conv_weight):
    import jax
    import jax.numpy as jnp

    def _L0_conv_ref(x, mag_w, mag_b, phase_w, phase_b, mag_gamma, mag_beta, mag_mean, mag_var, phase_gamma, phase_beta, phase_mean, phase_var, alpha):
        import jax, jax.numpy as jnp
        import numpy as np
        EPS = 1e-05

        def _bn(x, gamma, beta, mean, var):
            scale = gamma * jax.lax.rsqrt(var + EPS)
            return (x - mean[:, None, None]) * scale[:, None, None] + beta[:, None, None]

        def _prelu(x, alpha):
            a = alpha[0]
            return jnp.where(x >= 0, x, a * x)

        def _up2_nearest(x):
            return jnp.repeat(jnp.repeat(x, 2, axis=2), 2, axis=3)
        B, C, H, W = x.shape
        ph, pw = (H // 8, W // 8)
        nP = ph * pw
        p = x.reshape(B, C, ph, 8, pw, 8).transpose(0, 2, 4, 1, 3, 5).reshape(B * nP, C, 8, 8)
        low = p.reshape(B * nP, C, 4, 2, 4, 2).mean(axis=(3, 5))
        high = p - _up2_nearest(low)
        low = jnp.einsum('oc,nchw->nohw', mag_w, low) + mag_b[:, None, None]
        low = _prelu(_bn(low, mag_gamma, mag_beta, mag_mean, mag_var), alpha)
        hs = jnp.concatenate([high, jnp.roll(high, 1, axis=2)], axis=1)
        hs = jnp.einsum('oc,nchw->nohw', phase_w, hs) + phase_b[:, None, None]
        hs = _prelu(_bn(hs, phase_gamma, phase_beta, phase_mean, phase_var), alpha)
        high = hs[:, :C]
        out = _up2_nearest(low) + high
        out = out.reshape(B, ph, pw, C, 8, 8).transpose(0, 3, 1, 4, 2, 5).reshape(B, C, H, W)
        return out

    def _L1_conv_ref(x, cv1_w, cv1_b, scale_w, in_proj_w, conv_w, conv_b, x_proj_w, dt_w, dt_b, A_logs, Ds, ln_g, ln_b, out_proj_w, cv2_w, cv2_b):
        import jax, jax.numpy as jnp
        import numpy as np
        B, C1, C2, H, W = (4, 128, 128, 64, 64)
        Cm = int(C2 * 0.5)
        K = 4
        N = 1
        R = 8

        def conv1x1(x, w, b=None):
            y = jnp.einsum('bchw,oc->bohw', x, w)
            return y if b is None else y + b[None, :, None, None]

        def selective_scan(u, dt, A, Bs, Cs, Dsk):
            a = jnp.exp(dt[..., None] * A[None, :, :, None, :])
            b = (dt * u)[..., None] * Bs.transpose(0, 1, 3, 2)[:, :, None]

            def comb(e1, e2):
                a1, b1 = e1
                a2, b2 = e2
                return (a2 * a1, a2 * b1 + b2)
            _, h = jax.lax.associative_scan(comb, (a, b), axis=3)
            return jnp.einsum('bkdln,bknl->bkdl', h, Cs) + Dsk[None, :, :, None] * u

        def ss2d(xin, in_proj_w, conv_w, conv_b, x_proj_w, dt_w, dt_b, A_logs, Ds, ln_g, ln_b, out_proj_w):
            Bb, _, Hh, Ww = xin.shape
            L = Hh * Ww
            xz = conv1x1(xin, in_proj_w)
            xc, z = (xz[:, :Cm], xz[:, Cm:])
            z = jax.nn.silu(z)
            xc = jax.lax.conv_general_dilated(xc, conv_w, (1, 1), 'SAME', feature_group_count=Cm, dimension_numbers=('NCHW', 'OIHW', 'NCHW')) + conv_b[None, :, None, None]
            xc = jax.nn.silu(xc)
            xh = xc.reshape(Bb, Cm, L)
            xw = xc.transpose(0, 1, 3, 2).reshape(Bb, Cm, L)
            xs = jnp.stack([xh, xw, xh[..., ::-1], xw[..., ::-1]], axis=1)
            x_dbl = jnp.einsum('bkdl,kcd->bkcl', xs, x_proj_w)
            dts, Bs, Cs = jnp.split(x_dbl, [R, R + N], axis=2)
            dts = jnp.einsum('bkrl,kdr->bkdl', dts, dt_w)
            dt = jax.nn.softplus(dts + dt_b[None, :, :, None])
            A = -jnp.exp(A_logs).reshape(K, Cm, N)
            ys = selective_scan(xs, dt, A, Bs, Cs, Ds.reshape(K, Cm))
            y02 = ys[:, 0] + ys[:, 2, :, ::-1]
            y13 = ys[:, 1] + ys[:, 3, :, ::-1]
            y = y02.reshape(Bb, Cm, Hh, Ww) + y13.reshape(Bb, Cm, Ww, Hh).transpose(0, 1, 3, 2)
            mu = y.mean(axis=1, keepdims=True)
            var = y.var(axis=1, keepdims=True)
            y = (y - mu) / jnp.sqrt(var + 1e-05) * ln_g[None, :, None, None] + ln_b[None, :, None, None]
            y = y * z
            return conv1x1(y, out_proj_w)
        h = conv1x1(x, cv1_w, cv1_b)
        s = ss2d(h, in_proj_w, conv_w, conv_b, x_proj_w, dt_w, dt_b, A_logs, Ds, ln_g, ln_b, out_proj_w)
        s = scale_w * s
        return x + conv1x1(s, cv2_w, cv2_b)

    def _L2_conv_ref(x, cpe1_w, cpe1_b, n1_g, n1_b, inproj_w, inproj_b, actproj_w, actproj_b, dwc_w, dwc_b, qk_w, qk_b, lepe_w, lepe_b, outproj_w, outproj_b, cpe2_w, cpe2_b, n2_g, n2_b, fc1_w, fc1_b, fc2_w, fc2_b):
        import jax, jax.numpy as jnp
        import numpy as np
        B, DIM, H, W = (8, 128, 32, 32)
        HEADS = 8
        MLP_RATIO = 4.0

        def _dwconv(x, w, b):
            C = x.shape[1]
            y = jax.lax.conv_general_dilated(x, w, window_strides=(1, 1), padding='SAME', dimension_numbers=('NCHW', 'OIHW', 'NCHW'), feature_group_count=C)
            return y + b[None, :, None, None]

        def _ln(x, g, b):
            m = x.mean(-1, keepdims=True)
            v = ((x - m) ** 2).mean(-1, keepdims=True)
            return (x - m) * jax.lax.rsqrt(v + 1e-05) * g + b

        def _rope(x):
            bb, Hh, Ww, c = x.shape
            k_max = c // 4
            theta = 1.0 / 10000.0 ** (jnp.arange(k_max, dtype=x.dtype) / k_max)
            ah = jnp.arange(Hh, dtype=x.dtype)[:, None] * theta
            aw = jnp.arange(Ww, dtype=x.dtype)[:, None] * theta
            ang = jnp.concatenate([jnp.broadcast_to(ah[:, None, :], (Hh, Ww, k_max)), jnp.broadcast_to(aw[None, :, :], (Hh, Ww, k_max))], -1)
            cos, sin = (jnp.cos(ang), jnp.sin(ang))
            xr = x.reshape(bb, Hh, Ww, c // 2, 2)
            re, im = (xr[..., 0], xr[..., 1])
            out = jnp.stack([re * cos - im * sin, re * sin + im * cos], -1)
            return out.reshape(bb, Hh, Ww, c)

        def _attn(x, Hh, Ww, qk_w, qk_b, lepe_w, lepe_b):
            b, n, c = x.shape
            h = HEADS
            d = c // h
            qk = x @ qk_w + qk_b
            q = jax.nn.elu(qk[..., :c]) + 1.0
            k = jax.nn.elu(qk[..., c:]) + 1.0
            v = x
            qr = _rope(q.reshape(b, Hh, Ww, c)).reshape(b, n, h, d)
            kr = _rope(k.reshape(b, Hh, Ww, c)).reshape(b, n, h, d)
            qh = q.reshape(b, n, h, d)
            kh = k.reshape(b, n, h, d)
            vh = v.reshape(b, n, h, d)
            kmean = kh.mean(axis=1)
            z = 1.0 / (jnp.einsum('bnhd,bhd->bnh', qh, kmean) + 1e-06)
            kv = jnp.einsum('bnhd,bnhe->bhde', kr, vh) * (1.0 / n)
            out = jnp.einsum('bnhd,bhde->bnhe', qr, kv) * z[..., None]
            out = out.reshape(b, n, c)
            v2d = v.reshape(b, Hh, Ww, c).transpose(0, 3, 1, 2)
            lepe = _dwconv(v2d, lepe_w, lepe_b).transpose(0, 2, 3, 1).reshape(b, n, c)
            return out + lepe

        def _forward(x, cpe1_w, cpe1_b, n1_g, n1_b, inproj_w, inproj_b, actproj_w, actproj_b, dwc_w, dwc_b, qk_w, qk_b, lepe_w, lepe_b, outproj_w, outproj_b, cpe2_w, cpe2_b, n2_g, n2_b, fc1_w, fc1_b, fc2_w, fc2_b):
            Bb, C, Hh, Ww = x.shape
            n = Hh * Ww

            def tok2img(t):
                return t.reshape(Bb, Hh, Ww, C).transpose(0, 3, 1, 2)

            def img2tok(i):
                return i.transpose(0, 2, 3, 1).reshape(Bb, n, C)
            t = img2tok(x)
            t = t + img2tok(_dwconv(tok2img(t), cpe1_w, cpe1_b))
            shortcut = t
            tn = _ln(t, n1_g, n1_b)
            act_res = jax.nn.silu(tn @ actproj_w + actproj_b)
            ti = tn @ inproj_w + inproj_b
            ti = jax.nn.silu(img2tok(_dwconv(tok2img(ti), dwc_w, dwc_b)))
            ta = _attn(ti, Hh, Ww, qk_w, qk_b, lepe_w, lepe_b)
            t = shortcut + ta * act_res @ outproj_w + outproj_b
            t = t + img2tok(_dwconv(tok2img(t), cpe2_w, cpe2_b))
            tn2 = _ln(t, n2_g, n2_b)
            mlp = jax.nn.gelu(tn2 @ fc1_w + fc1_b, approximate=False) @ fc2_w + fc2_b
            t = t + mlp
            return tok2img(t)
        return _forward(x, cpe1_w, cpe1_b, n1_g, n1_b, inproj_w, inproj_b, actproj_w, actproj_b, dwc_w, dwc_b, qk_w, qk_b, lepe_w, lepe_b, outproj_w, outproj_b, cpe2_w, cpe2_b, n2_g, n2_b, fc1_w, fc1_b, fc2_w, fc2_b)

    def _L3_conv_ref(x, weight):
        import jax, jax.numpy as jnp
        import numpy as np
        STRIDE = 1
        PADDING = 1

        def _binary_activation(x):
            out_forward = jnp.sign(x)
            m1 = (x < -1).astype(x.dtype)
            m2 = (x < 0).astype(x.dtype)
            m3 = (x < 1).astype(x.dtype)
            out1 = -1.0 * m1 + (x * x + 2.0 * x) * (1.0 - m1)
            out2 = out1 * m2 + (-x * x + 2.0 * x) * (1.0 - m2)
            out3 = out2 * m3 + 1.0 * (1.0 - m3)
            return jax.lax.stop_gradient(out_forward) - jax.lax.stop_gradient(out3) + out3

        def _binary_weights(w):
            scaling = jax.lax.stop_gradient(jnp.mean(jnp.abs(w), axis=(1, 2, 3), keepdims=True))
            bw_no_grad = scaling * jnp.sign(w)
            clipped = jnp.clip(w, -1.0, 1.0)
            return jax.lax.stop_gradient(bw_no_grad) - jax.lax.stop_gradient(clipped) + clipped
        bw = _binary_weights(weight)
        ba = _binary_activation(x)
        y = jax.lax.conv_general_dilated(ba, bw, window_strides=(STRIDE, STRIDE), padding=[(PADDING, PADDING), (PADDING, PADDING)], dimension_numbers=('NCHW', 'OIHW', 'NCHW'))
        return y

    def _gn(v, G=32, eps=1e-05):
        B_, C_, H_, W_ = v.shape
        g = v.reshape(B_, G, C_ // G, H_, W_)
        m = jnp.mean(g, axis=(2, 3, 4), keepdims=True)
        s = jnp.var(g, axis=(2, 3, 4), keepdims=True)
        return ((g - m) / jnp.sqrt(s + eps)).reshape(v.shape)

    def _ln_c(v, eps=1e-06):
        m = jnp.mean(v, axis=1, keepdims=True)
        s = jnp.var(v, axis=1, keepdims=True)
        return (v - m) / jnp.sqrt(s + eps)

    def _ln_t(v, eps=1e-05):
        m = jnp.mean(v, axis=-1, keepdims=True)
        s = jnp.var(v, axis=-1, keepdims=True)
        return (v - m) / jnp.sqrt(s + eps)

    def _to_tokens(v):
        B_, C_, H_, W_ = v.shape
        return v.reshape(B_, C_, H_ * W_).transpose(0, 2, 1)

    def _from_tokens(t, like):
        B_, C_, H_, W_ = like.shape
        return t.transpose(0, 2, 1).reshape(B_, C_, H_, W_)
    x = _L0_conv_ref(x, L0_conv_mag_w, L0_conv_mag_b, L0_conv_phase_w, L0_conv_phase_b, L0_conv_mag_gamma, L0_conv_mag_beta, L0_conv_mag_mean, L0_conv_mag_var, L0_conv_phase_gamma, L0_conv_phase_beta, L0_conv_phase_mean, L0_conv_phase_var, L0_conv_alpha)
    x = _L1_conv_ref(x, L1_conv_cv1_w, L1_conv_cv1_b, L1_conv_scale_w, L1_conv_in_proj_w, L1_conv_conv_w, L1_conv_conv_b, L1_conv_x_proj_w, L1_conv_dt_w, L1_conv_dt_b, L1_conv_A_logs, L1_conv_Ds, L1_conv_ln_g, L1_conv_ln_b, L1_conv_out_proj_w, L1_conv_cv2_w, L1_conv_cv2_b)
    x = _L2_conv_ref(x, L2_conv_cpe1_w, L2_conv_cpe1_b, L2_conv_n1_g, L2_conv_n1_b, L2_conv_inproj_w, L2_conv_inproj_b, L2_conv_actproj_w, L2_conv_actproj_b, L2_conv_dwc_w, L2_conv_dwc_b, L2_conv_qk_w, L2_conv_qk_b, L2_conv_lepe_w, L2_conv_lepe_b, L2_conv_outproj_w, L2_conv_outproj_b, L2_conv_cpe2_w, L2_conv_cpe2_b, L2_conv_n2_g, L2_conv_n2_b, L2_conv_fc1_w, L2_conv_fc1_b, L2_conv_fc2_w, L2_conv_fc2_b)
    x = _L3_conv_ref(x, L3_conv_weight)
    return x

_drawn_inputs = setup_inputs


def setup_inputs(seed=0):
    import zlib

    import numpy as np

    out = dict(_drawn_inputs(seed))
    spreads = {'L0_conv_mag_gamma': (1.0, 0.6),
     'L0_conv_mag_beta': (0.0, 0.1),
     'L0_conv_phase_gamma': (1.0, 0.6),
     'L0_conv_phase_beta': (0.0, 0.36),
     'L1_conv_scale_w': (0.10000000149011612, 0.6),
     'L1_conv_Ds': (1.0, 0.6),
     'L1_conv_ln_g': (1.0, 0.6),
     'L1_conv_ln_b': (0.0, 0.8),
     'L2_conv_cpe1_b': (0.0, 0.1),
     'L2_conv_n1_g': (1.0, 0.6),
     'L2_conv_n1_b': (0.0, 0.8),
     'L2_conv_inproj_b': (0.0, 0.8),
     'L2_conv_actproj_b': (0.0, 0.8),
     'L2_conv_dwc_b': (0.0, 0.8),
     'L2_conv_qk_b': (0.0, 0.8),
     'L2_conv_lepe_b': (0.0, 0.8),
     'L2_conv_outproj_b': (0.0, 0.1),
     'L2_conv_cpe2_b': (0.0, 0.1),
     'L2_conv_n2_g': (1.0, 0.6),
     'L2_conv_n2_b': (0.0, 0.8),
     'L2_conv_fc1_b': (0.0, 0.444),
     'L2_conv_fc2_b': (0.0, 0.1)}
    factors = {'L0_conv_mag_b': 8.0,
     'L0_conv_phase_b': 8.0,
     'L0_conv_mag_var': 3.912,
     'L0_conv_phase_mean': 2.682,
     'L0_conv_phase_var': 3.712,
     'L1_conv_cv1_w': 3.694,
     'L1_conv_cv1_b': 8.0,
     'L1_conv_in_proj_w': 3.581,
     'L1_conv_conv_w': 3.838,
     'L1_conv_conv_b': 5.728,
     'L1_conv_x_proj_w': 8.0,
     'L1_conv_dt_w': 8.0,
     'L1_conv_dt_b': 8.0,
     'L1_conv_A_logs': 8.0,
     'L1_conv_out_proj_w': 3.743,
     'L1_conv_cv2_w': 3.616,
     'L2_conv_cpe1_w': 3.118,
     'L2_conv_inproj_w': 8.0,
     'L2_conv_actproj_w': 8.0,
     'L2_conv_dwc_w': 8.0,
     'L2_conv_qk_w': 8.0,
     'L2_conv_lepe_w': 8.0,
     'L2_conv_outproj_w': 8.0,
     'L2_conv_cpe2_w': 3.213,
     'L2_conv_fc1_w': 2.733,
     'L3_conv_weight': 3.726}
    for name, (base, spread) in spreads.items():
        noise = np.random.default_rng([zlib.crc32(name.encode()), seed]).standard_normal(out[name].shape)
        drawn = base * np.exp(spread * noise) if base else spread * noise
        out[name] = jnp.asarray(drawn.astype(out[name].dtype))
    for name, factor in factors.items():
        out[name] = (out[name] * factor).astype(out[name].dtype)
    return out
```

```python
from contextlib import ExitStack

import numpy as np

import concourse.bass as bass
from concourse import mybir

F32 = mybir.dt.float32
BF16 = mybir.dt.bfloat16
ACT = mybir.ActivationFunctionType
ALU = mybir.AluOpType
ds = bass.ds

P = 128
CM = 64
ROWS = 8
HALF = ROWS // 2
BANK = 512
CREDIT = 2
HEADS = 8
RANK = 8
EPS = 1e-5
CAP = 40.0

TAPS = [(0, 0), (0, -1), (0, 1), (-1, 0), (1, 0), (-1, -1), (-1, 1), (1, -1), (1, 1)]
VECTOR_TAPS = {"cpe1": 6, "dwc": 6, "lepe": 5, "cpe2": 6}


HOST_COLS = ["mag_b", "mag_gamma", "mag_beta", "mag_mean", "mag_var", "ph_b", "ph_gamma", "ph_beta", "ph_mean", "ph_var",
             "alpha", "l1_dtb0", "l1_dtb1", "l1_A0", "l1_A1", "l1_gb", "l1_scale", "l1_cb", "l1_cv1b", "cv2_b",
             "cpe1_b", "n1_g", "n1_b", "in_b", "act_b", "dwc_b", "q_b", "lepe_b", "out_b", "cpe2_b", "n2_g", "n2_b",
             "fc2_b", "fc1_b", "taps", "l1taps", "l1_D"]
CHIP_COLS = ["fc1_o", "mag_s", "mag_o", "mag_ns", "mag_no", "ph_s", "ph_o", "ph_ns", "ph_no", "nalpha", "xc_b", "z_b",
             "in_o", "act_o", "q_b1", "w3_s", "ksum", "zero", "one", "eps", "tiny", "Dsum", "root", "root2"]


def tap_column(tap):
    return 3 * (tap[0] + 1) + tap[1] + 1


def pipelined(eng, count, stages):
    deepest = max(lag for lag, _ in stages)

    def step(t, parity, whole):
        for lag, stage in stages:
            if whole or 0 <= t - lag < count:
                stage(t - lag, (parity - lag) % 2)

    start = deepest + 1
    pairs = (count - start) // 2
    for t in range(min(start, count)):
        step(t, t % 2, False)
    if pairs >= 2:
        with eng.Fori(0, pairs, 1) as k:
            for u in range(2):
                step(2 * k + (start + u), (start + u) % 2, True)
        start += 2 * pairs
    for t in range(start, count + deepest):
        step(t, t % 2, False)


def build(nc, t, out):
    B, _, S, _ = t["x"].shape
    NB = S // ROWS
    N = S * S
    BLK = ROWS * S
    HC = HALF * S
    SP = S + 2
    NT = BLK // P
    REGION = max(SP * SP, 25 * BLK // 2)
    QUARTER = BLK // 4

    def done(i, b):
        return i * NB + (b + (1 + CREDIT))

    def steps(i, b, each, step):
        return i * (NB * each) + (b * each + step)

    def landed(i, b, p):
        return i * (8 * NB) + (b * 8 + (16 - 8 * p))

    ctx = ExitStack()
    with ctx:
        def sb(name, shape, dt=F32):
            return ctx.enter_context(nc.sbuf_tensor(name, shape, dt))

        def sem(name):
            return ctx.enter_context(nc.semaphore(name))

        psum = ctx.enter_context(nc.psum_tensor("psum", [P, 8, BANK], F32))

        def pair(bank):
            return psum[:, bank:bank + 2, 0:HC]

        def rows_of(ap):
            return ap.rearrange("p a (r w) -> p a r w", w=S)

        R = [sb(f"region{k}", [P, REGION]) for k in range(4)]

        def padded(k):
            return R[k][:, 0:SP * SP].rearrange("p (h w) -> p h w", w=SP)

        def flat(k, b):
            return R[k][:, ds(BLK * b, BLK)]

        def prow(k, b, dh=0, dw=0, rows=ROWS, skip=0):
            return padded(k)[:, ds(ROWS * b + (1 + dh + skip), rows), 1 + dw:1 + dw + S]

        work = sb("work", [P, 8 * BLK])

        def tile(n):
            return work[:, n * BLK:(n + 1) * BLK]

        def region_tile(k, n):
            return R[k][:, n * BLK:(n + 1) * BLK]

        def halves(ap):
            return ap.rearrange("p (a c) -> p a c", a=2)

        def by_rows(ap):
            return ap.rearrange("p (a r w) -> p a r w", a=2, w=S)

        names = {}

        def mat(name, cols=P, rows=P, dt=F32):
            names[name] = sb("m_" + name, [rows, cols], dt)
            return names[name]

        ident = mat("ident")
        cen128 = mat("cen128")
        avg128 = mat("avg128")
        headmask = mat("headmask")
        rot = mat("rot")
        rotT = mat("rotT")
        ph_a, ph_b, magT = mat("ph_a"), mat("ph_b"), mat("magT")
        w_xc, w_z = mat("w_xc"), mat("w_z")
        dwl1 = [mat(f"dwl1_{n}") for n in range(6)]
        w_dt = [mat(f"w_dt{n}") for n in range(2)]
        w_B = [mat(f"w_B{n}") for n in range(2)]
        w_C = [mat(f"w_C{n}") for n in range(2)]
        cen64, cen64_up, cen64_d = mat("cen64"), mat("cen64_up"), mat("cen64_d")
        w_l1out = mat("w_l1out")
        convs = ("cpe1", "dwc", "lepe", "cpe2")
        diag = {c: [mat(f"{c}_{n}") for n in range(9 - VECTOR_TAPS[c])] for c in convs}
        w_in, w_act, w_q, w_out = mat("w_in"), mat("w_act"), mat("w_q"), mat("w_out")
        w_ki = mat("w_ki", 2 * P)
        kbias = mat("kbias")
        kv, kv_rot, kmean = mat("kv"), mat("kv_rot"), mat("kmean")
        fc1 = mat("fc1", 4 * P)
        fc2 = mat("fc2", 4 * P)
        w3 = mat("w3", 9 * P, dt=BF16)

        groups = {"fc1_b": 4, "taps": 36, "l1taps": 6, "l1_D": 4, "fc1_o": 4}
        at, width = {}, 0
        for name in HOST_COLS + CHIP_COLS:
            at[name] = width
            width += groups[name] if name in groups else 1
        host_width = at[CHIP_COLS[0]]
        cols = sb("cols", [P, width])

        def col(name, n=0, rows=slice(0, P)):
            return cols[rows, at[name] + n:at[name] + n + 1]

        def tap_weight(conv, tap):
            return col("taps", 9 * convs.index(conv) + tap_column(tap))

        block_signals = []

        def signal(name, owner):
            s = sem(name)
            block_signals.append((s, owner))
            return s

        setup_loaded = sem("setup_loaded")
        late_loaded = sem("late_loaded")
        setup_vec = sem("setup_vec")
        setup_act = sem("setup_act")
        setup_pe = sem("setup_pe")
        ready = sem("ready")

        x_in = [sem(f"x_in{n}") for n in range(2)]
        l0_high = signal("l0_high", "v")
        l0_mm = signal("l0_mm", "p")
        l0_relu = signal("l0_relu", "a")
        l0_out = signal("l0_out", "v")
        a_mm = signal("a_mm", "p")
        a_xc = signal("a_xc", "v")
        a_act = signal("a_act", "a")
        b_mm = signal("b_mm", "p")
        b_act = signal("b_act", "a")
        c_sets = []
        for d in "fr":
            c_sets.append({k: signal(f"c{d}_{k}", o) for k, o in (
                ("dt", "p"), ("B", "p"), ("C", "p"), ("cap", "v"), ("exp", "a"), ("log", "a"), ("step", "v"), ("decay", "a"),
                ("du", "g"), ("bu", "v"), ("h", "v"), ("hc", "v"), ("y", "g")) if d + k != "fy"})
        d_yc = signal("d_yc", "p")
        d_sq = signal("d_sq", "a")
        d_var = signal("d_var", "p")
        d_log = signal("d_log", "a")
        d_rstd = signal("d_rstd", "a")
        d_norm = signal("d_norm", "v")
        d_gate = signal("d_gate", "g")
        d_mm = signal("d_mm", "p")
        d_out = signal("d_out", "v")
        n_sets = []
        for d in ("e", "g"):
            n_sets.append({k: signal(f"{d}1_{k}", o) for k, o in (
                ("conv", "p"), ("t", "v"), ("yc", "p"), ("sq", "a"), ("var", "p"), ("log", "a"), ("rstd", "a"), ("tn", "v"))})
        e2_mm = signal("e2_mm", "p")
        e2_ti = signal("e2_ti", "v")
        e2_act = signal("e2_act", "a")
        e2_conv = signal("e2_conv", "p")
        e2_sum = signal("e2_sum", "v")
        e2_v = signal("e2_v", "a")
        f1_stage = signal("f1_stage", "g")
        f1_mm = signal("f1_mm", "p")
        f1_bias = signal("f1_bias", "v")
        f1_min = signal("f1_min", "v")
        f1_exp = signal("f1_exp", "a")
        f1_vT = signal("f1_vT", "a")
        f1_k = signal("f1_k", "v")
        f1_kc = signal("f1_kc", "g")
        f1_ks = signal("f1_ks", "v")
        f1_kv = signal("f1_kv", "p")
        f1_ksum = signal("f1_ksum", "g")
        f1_tab = [sem(f"f1_tab{n}") for n in range(2)]
        image_begun = sem("image_begun")
        kv_pe = sem("kv_pe")
        kv_vec = sem("kv_vec")
        f2_q = signal("f2_q", "p")
        f2_min = signal("f2_min", "v")
        f2_exp = signal("f2_exp", "a")
        f2_phi = signal("f2_phi", "v")
        f2_qc = signal("f2_qc", "g")
        f2_qs = signal("f2_qs", "v")
        f2_den = signal("f2_den", "p")
        f2_log = signal("f2_log", "a")
        f2_z = signal("f2_z", "a")
        f2_num = signal("f2_num", "p")
        f2_nz = signal("f2_nz", "v")
        f2_conv = signal("f2_conv", "p")
        f2_lepe = signal("f2_lepe", "v")
        f2_sum = signal("f2_sum", "g")
        f2_ta = signal("f2_ta", "g")
        f2_out = signal("f2_out", "p")
        f2_t2 = signal("f2_t2", "v")
        f2_tab = [sem(f"f2_tab{n}") for n in range(2)]
        g2_fc1 = signal("g2_fc1", "p")
        g2_gelu = signal("g2_gelu", "a")
        g2_fc2 = signal("g2_fc2", "p")
        g2_x3 = signal("g2_x3", "v")
        g2_sign = signal("g2_sign", "a")
        h_mm = signal("h_mm", "p")
        h_scale = signal("h_scale", "a")
        h_store = [sem(f"h_store{n}") for n in range(2)]
        borders = sem("borders")
        tap_steps = {c: sem(f"{c}_tap_steps") for c in convs}
        l0_steps = sem("l0_steps")
        l0_join = sem("l0_join")
        setup_steps = sem("setup_steps")

        def credit(eng, owner):
            for s, o in block_signals:
                if o == owner:
                    eng.sem_inc(s, CREDIT * (4 if s is g2_fc1 or s is g2_gelu else 1))

        def all_done(eng, i, *signals):
            eng.wait_ge(ready, 1)
            for s in signals:
                k = 4 if s is g2_fc1 or s is g2_gelu else 1
                eng.wait_ge(s, i * (NB * k) + (NB + CREDIT) * k)

        L0_ALL = (l0_high, l0_mm, l0_relu, l0_out)
        A_ALL = (a_mm, a_xc, a_act)
        B_ALL = (b_mm, b_act)
        C_ALL = [tuple(c.values()) for c in c_sets]
        D_ALL = (d_yc, d_sq, d_var, d_log, d_rstd, d_norm, d_gate, d_mm, d_out)
        N_ALL = [tuple(c.values()) for c in n_sets]
        E2_ALL = (e2_mm, e2_ti, e2_act, e2_conv, e2_sum, e2_v)
        F1_ALL = (f1_stage, f1_mm, f1_bias, f1_min, f1_exp, f1_vT, f1_k, f1_kc, f1_ks, f1_kv, f1_ksum)
        F2_ALL = (f2_q, f2_min, f2_exp, f2_phi, f2_qc, f2_qs, f2_den, f2_log, f2_z, f2_num, f2_nz, f2_conv, f2_lepe, f2_sum, f2_ta,
                  f2_out, f2_t2)
        G2_ALL = (g2_fc1, g2_gelu, g2_fc2, g2_x3, g2_sign)
        H_ALL = (h_mm, h_scale)

        rhs_l1 = R[0][0:CM, 0:4 * CM]
        cv1 = R[0][0:CM, 256:384]
        opj2 = R[0][0:CM, 384:512]
        cv2T = R[0][0:CM, 512:640]
        cv2Ts = R[0][0:CM, 640:768]
        xp_r = R[1][0:RANK, 0:4 * P]
        dt_r = R[1][0:RANK, 512:512 + 4 * P]
        bc_r = R[1][0:2, 1024:1024 + 4 * P]
        half_ones = R[1][0:2, 1536:1664]
        ones_row = R[1][0:1, 1664:1792]
        kb_row = R[1][0:1, 1792:1920]
        w3_nat = R[2][:, 0:9 * P]
        w3_T = R[2][:, 9 * P:18 * P]
        e2mask = R[3][:, 0:P]
        raw_in = R[3][:, 128:256]
        raw_act = R[3][:, 256:384]
        raw_fc1 = R[3][:, 384:896]
        loads = [
            (ident[:, :], t["c_ident"]), (cen128[:, :], t["c_cen128"]), (avg128[:, :], t["c_avg128"]),
            (headmask[:, :], t["c_headmask"]), (rot[:, :], t["c_rot"]), (rotT[:, :], t["c_rotT"]),
            (cen64[:, :], t["c_cen64"]), (cen64_up[:, :], t["c_cen64_up"]), (e2mask, t["c_e2"]),
            (ph_a[:, :], t["ph_aT"]), (ph_b[:, :], t["ph_bT"]), (magT[:, :], t["magT"]),
            (rhs_l1[:, 0:64], t["inprojT"][:, 0:64]), (rhs_l1[:, 64:128], t["inprojT"][:, 0:64]),
            (rhs_l1[:, 128:192], t["inprojT"][:, 64:128]), (rhs_l1[:, 192:256], t["inprojT"][:, 64:128]),
            (cv1, t["cv1_w"]), (opj2[:, 0:64], t["out_proj"]), (opj2[:, 64:128], t["out_proj"]), (cv2T, t["cv2T"]),
            (raw_in, t["inproj_w"]), (raw_act, t["actproj_w"]), (raw_fc1, t["fc1_w"]),
            (fc2[:, :].rearrange("p (j o) -> p j o", j=4), t["fc2_w"].rearrange("(j p) o -> p j o", p=P)),
            (w_q[:, :], t["qk_w"][:, 0:P]), (w_ki[:, 0:P], t["qk_w"][:, P:2 * P]), (w_ki[:, P:2 * P], t["c_ident"]),
            (w_out[:, :], t["outproj_w"]), (kb_row, t["kb_row"]), (half_ones, t["c_half"]),
            (w3_nat, t["w3_nat"]), (w3_T, t["w3_T"]),
            (cols[:, 0:host_width], t["cols"]),
        ]
        late_loads = []
        for k in range(4):
            lo, hi = P * k + CM * (k % 2), P * k + CM * (k % 2) + CM
            late_loads.append((xp_r[:, lo:hi], t["x_proj"][k, 0:RANK, :]))
            late_loads.append((dt_r[:, lo:hi], t["dt_wT"][k]))
        for sweep in range(2):
            for half in range(2):
                for what in range(2):
                    c0 = P * (2 * sweep + what) + CM * half
                    late_loads.append((bc_r[half:half + 1, c0:c0 + CM],
                                       t["x_proj"][2 * sweep + half, RANK + what:RANK + what + 1, :]))


        def kcs(p):
            return R[3][:, (2 + 2 * p) * BLK:(4 + 2 * p) * BLK].rearrange("p (n c) -> p n c", n=NT)

        def tok_table(p, which):
            v = region_tile(3, 6 + p).rearrange("p (s n j) -> p s n j", s=2, n=NT)[:, which]
            return v.unsqueeze(3).broadcast_to((P, NT, CM, 2))

        def by_pairs(ap):
            return ap.rearrange("p n (j e) -> p n j e", e=2)

        def by_tile(ap):
            return ap.rearrange("p (n c) -> p n c", n=NT)

        def signs():
            return R[1][:, :].bitcast(BF16)[:, 0:SP * SP].rearrange("p (h w) -> p h w", w=SP)

        def pad_rows(k, b, parts, up=0):
            return padded(k)[parts, ds(ROWS * b + (1 - up), ROWS), 1:1 + S].rearrange("p (a r) w -> p a r w", a=2)

        def token_psum(p):
            v = psum[:, 3 * p:3 * p + 3, :].rearrange("p a c -> p (a c)")[:, 0:NT * 2 * P]
            return v.rearrange("p (n c) -> p n c", c=2 * P)

        def quarter(n):
            return R[2][:, n * QUARTER:(n + 1) * QUARTER]

        x_tile = [region_tile(2, p) for p in range(2)]
        pair_sum = [R[2][:, (8 + 2 * p) * QUARTER:(10 + 2 * p) * QUARTER] for p in range(2)]
        quad_sum = [quarter(12 + p) for p in range(2)]
        low_pos = [quarter(14 + p) for p in range(2)]
        low_wide = [R[2][:, (16 + 2 * p) * QUARTER:(18 + 2 * p) * QUARTER] for p in range(2)]
        high = [R[2][:, 5 * BLK + p * 9 * S:5 * BLK + (p + 1) * 9 * S].rearrange("p (r w) -> p r w", w=S)
                for p in range(2)]
        hs_pos = [R[2][:, (30 + 4 * p) * QUARTER:(34 + 4 * p) * QUARTER] for p in range(2)]
        hs_neg = [R[2][:, (38 + 4 * p) * QUARTER:(42 + 4 * p) * QUARTER] for p in range(2)]
        low_neg = [quarter(46 + p) for p in range(2)]
        out_low = R[2][:, 48 * QUARTER:50 * QUARTER]

        def sweep_block(sweep, b):
            return b if sweep == 0 else b * (-1) + (NB - 1)

        block = ctx.enter_context(nc.Block())

        @block.sync
        def _(sp):
            for dst, src in loads:
                sp.dma_start(dst, src).then_inc(setup_loaded, 16)
            sp.wait_ge(setup_vec, 1)
            for dst, src in late_loads:
                sp.dma_start(dst, src).then_inc(late_loaded, 16)
            for p in range(2):
                sp.sem_inc(h_store[p], 16)
            sp.wait_ge(ready, 1)
            with sp.Fori(0, B, 1) as i:
                def load_x(b, p):
                    sp.wait_ge(ready, 1)
                    sp.wait_ge(l0_high, done(i, b - 2))
                    sp.dma_start(x_tile[p], t["x"][ds(i, 1), :, ds(ROWS * b, ROWS), :]
                                 .rearrange("a c h w -> (a c) (h w)")).then_inc(x_in[p], 16)

                def load_tok_table(b, p):
                    sp.wait_ge(ready, 1)
                    sp.wait_ge(f1_kc, done(i, b - 2))
                    sp.wait_ge(f1_ks, done(i, b - 2))
                    sp.dma_start(region_tile(3, 6 + p), t["tab_tok"][ds(b, 1), :, :].rearrange("a p n -> (a p) n"))\
                        .then_inc(f1_tab[p], 16)

                def load_ch_table(b, p):
                    sp.wait_ge(ready, 1)
                    sp.wait_ge(f2_qc, done(i, b - 2))
                    sp.wait_ge(f2_qs, done(i, b - 2))
                    sp.dma_start(R[3][:, 2 * p * BLK:(2 * p + 2) * BLK],
                                 t["tab_ch"][ds(b, 1), :, :].rearrange("a p n -> (a p) n")).then_inc(f2_tab[p], 16)

                def store(b, p):
                    sp.wait_ge(ready, 1)
                    sp.wait_ge(h_scale, done(i, b))
                    sp.dma_start(out[ds(i, 1), :, ds(ROWS * b, ROWS), :].rearrange("a c h w -> (a c) (h w)"),
                                 tile(p)).then_inc(h_store[p], 16)

                all_done(sp, i - 1, *G2_ALL)
                pipelined(sp, NB, [(0, load_x)])
                all_done(sp, i, *E2_ALL)
                pipelined(sp, NB, [(0, load_tok_table)])
                all_done(sp, i, *F1_ALL)
                pipelined(sp, NB, [(0, load_ch_table)])
                pipelined(sp, NB, [(0, store)])
            for p in range(2):
                sp.wait_ge(h_store[p], 16 + B * NB // 2 * 16)

        @block.gpsimd
        def _(g):
            credit(g, "g")
            g.wait_ge(ready, 1)
            with g.Fori(0, B, 1) as i:
                def clear_frame(image, last=1):
                    g.memset(image[:, 0:1, :], 0.0)
                    g.memset(image[:, SP - last:SP, :], 0.0)
                    g.memset(image[:, 1:SP - last, 0:1], 0.0)
                    g.memset(image[:, 1:SP - last, SP - 1:SP], 0.0).then_inc(borders, 1)

                all_done(g, i - 1, *G2_ALL)
                g.sem_inc(image_begun, 1)
                clear_frame(padded(3), last=2)

                for sweep in range(2):
                    c = c_sets[sweep]

                    def du(b, p):
                        g.wait_ge(ready, 1)
                        g.wait_ge(c["step"], done(i, b))
                        g.wait_ge(c["h"], done(i, b - 2))
                        g.tensor_tensor(tile(2 + p), tile(p), flat(2, sweep_block(sweep, b)), ALU.mult)\
                            .then_inc(c["du"], 1)

                    def add_y(b, p):
                        y = flat(3, sweep_block(sweep, b))
                        g.wait_ge(ready, 1)
                        g.wait_ge(c["hc"], done(i, b))
                        g.tensor_tensor(y, y, tile(4 + p), ALU.add).then_inc(c["y"], 1)

                    if sweep == 0:
                        all_done(g, i, *B_ALL)
                        pipelined(g, NB, [(0, du)])
                    else:
                        all_done(g, i, *C_ALL[0])
                        pipelined(g, NB, [(0, du), (2, add_y)])

                def gate(b, p):
                    z = flat(1, b)[0:CM]
                    g.wait_ge(ready, 1)
                    g.wait_ge(d_norm, done(i, b))
                    g.tensor_tensor(z, tile(2 + p)[0:CM], z, ALU.mult).then_inc(d_gate, 1)

                all_done(g, i, *C_ALL[1])
                pipelined(g, NB, [(0, gate)])

                all_done(g, i, *D_ALL)
                clear_frame(padded(1))
                clear_frame(padded(3))

                def stage(b, p):
                    g.wait_ge(ready, 1)
                    g.wait_ge(f1_mm, done(i, b - 2))
                    g.tensor_copy(region_tile(3, p).rearrange("p (r w) -> p r w", w=S), prow(0, b))\
                        .then_inc(f1_stage, 1)

                def kc(b, p):
                    g.wait_ge(ready, 1)
                    g.wait_ge(f1_k, done(i, b))
                    g.wait_ge(f1_tab[p], landed(i, b, p))
                    g.wait_ge(f1_kv, done(i, b - 2))
                    g.tensor_tensor(by_pairs(kcs(p)[:, :, 0:P]), by_pairs(by_tile(tile(p))), tok_table(p, 0), ALU.mult)\
                        .then_inc(f1_kc, 1)

                def ksum(b, p):
                    if isinstance(b, int) and b == 0:
                        g.tensor_copy(tile(6), tile(p)).then_inc(f1_ksum, 1)
                    else:
                        g.wait_ge(ready, 1)
                        g.wait_ge(f1_ksum, done(i, b - 1))
                        g.tensor_tensor(tile(6), tile(6), tile(p), ALU.add).then_inc(f1_ksum, 1)

                all_done(g, i, *E2_ALL)
                pipelined(g, NB, [(0, stage), (1, kc), (1, ksum)])

                def qc(b, p):
                    g.wait_ge(ready, 1)
                    g.wait_ge(f2_phi, done(i, b))
                    g.wait_ge(f2_tab[p], landed(i, b, p))
                    g.wait_ge(f2_num, done(i, b - 2))
                    g.tensor_tensor(region_tile(3, 4 + p), tile(p), region_tile(3, 2 * p), ALU.mult).then_inc(f2_qc, 1)

                def ta(b, p):
                    g.wait_ge(ready, 1)
                    g.wait_ge(f2_nz, done(i, b))
                    g.wait_ge(f2_lepe, done(i, b))
                    g.tensor_tensor(tile(4 + p), tile(4 + p), tile(2 + p), ALU.add).then_inc(f2_sum, 1)
                    g.wait_ge(ready, 1)
                    g.wait_ge(f2_sum, done(i, b))
                    g.tensor_tensor(tile(4 + p), tile(4 + p), flat(2, b), ALU.mult).then_inc(f2_ta, 1)

                all_done(g, i, *F1_ALL)
                pipelined(g, NB, [(0, qc), (1, ta)])

                all_done(g, i, *N_ALL[1])
                clear_frame(signs())

        @block.scalar
        def _(a):
            credit(a, "a")
            a.wait_ge(setup_loaded, 16 * len(loads))
            a.wait_ge(setup_vec, 2)
            a.activation(col("root"), col("mag_var"), ACT.Sqrt, bias=col("eps"))
            a.activation(col("root2"), col("ph_var"), ACT.Sqrt, bias=col("eps"))
            a.activation(w3[:, :], w3_T, ACT.Sign)
            a.activation(w3_nat, w3_nat, ACT.Abs, accum_out=col("w3_s"))
            a.activation(col("l1_A0"), col("l1_A0"), ACT.Exp)
            a.activation(col("l1_A1"), col("l1_A1"), ACT.Exp).then_inc(setup_act, 1)
            a.wait_ge(ready, 1)
            with a.Fori(0, B, 1) as i:
                def relus(b, p):
                    a.wait_ge(ready, 1)
                    a.wait_ge(l0_mm, done(i, b))
                    a.wait_ge(l0_out, done(i, b - 2))
                    low = psum[:, 4 + p, 0:QUARTER]
                    a.activation(low_pos[p], low, ACT.Relu, bias=col("mag_o"), scale=col("mag_s"))
                    a.activation(low_neg[p], low, ACT.Relu, bias=col("mag_no"), scale=col("mag_ns"))
                    a.activation(halves(hs_pos[p]), pair(2 * p), ACT.Relu, bias=col("ph_o"), scale=col("ph_s"))
                    a.activation(halves(hs_neg[p]), pair(2 * p), ACT.Relu, bias=col("ph_no"), scale=col("ph_ns"))\
                        .then_inc(l0_relu, 1)

                pipelined(a, NB, [(0, relus)])

                def silu_z(b, p):
                    a.wait_ge(ready, 1)
                    a.wait_ge(a_mm, done(i, b))
                    a.activation(pad_rows(3, b, slice(CM, P), up=1), rows_of(pair(2 * p))[CM:P], ACT.Identity,
                                 bias=col("xc_b", rows=slice(CM, P)))
                    a.activation(halves(flat(1, b)), pair(4 + 2 * p), ACT.Silu, bias=col("z_b")).then_inc(a_act, 1)

                a.wait_ge(borders, i * 4 + 1)
                all_done(a, i, *L0_ALL)
                pipelined(a, NB, [(0, silu_z)])

                def silu_u(b, p):
                    a.wait_ge(ready, 1)
                    a.wait_ge(b_mm, done(i, b))
                    a.activation(halves(flat(2, b)[0:CM]), pair(2 * p)[0:CM], ACT.Silu, bias=col("l1_cb", rows=slice(0, CM)))
                    turned = R[2][CM:P, 0:N].rearrange("p (w h) -> p h w", h=S)[:, ds(ROWS * b, ROWS), :]
                    a.activation(turned.rearrange("p (a r) w -> p a r w", a=2), rows_of(pair(2 * p))[CM:P], ACT.Silu,
                                 bias=col("l1_cb", rows=slice(CM, P))).then_inc(b_act, 1)

                all_done(a, i, *A_ALL)
                pipelined(a, NB, [(0, silu_u)])

                for sweep in range(2):
                    c = c_sets[sweep]

                    def soft(b, p):
                        a.wait_ge(ready, 1)
                        a.wait_ge(c["cap"], done(i, b))
                        a.activation(tile(p), tile(p), ACT.Exp).then_inc(c["exp"], 1)
                        a.wait_ge(ready, 1)
                        a.wait_ge(c["exp"], done(i, b))
                        a.activation(tile(p), tile(p), ACT.Ln, bias=col("one")).then_inc(c["log"], 1)

                    def decay(b, p):
                        a.wait_ge(ready, 1)
                        a.wait_ge(c["step"], done(i, b))
                        a.wait_ge(c["hc" if sweep == 0 else "y"], done(i, b - 2))
                        a.activation(tile(4 + p), tile(p), ACT.Exp, scale=col(f"l1_A{sweep}")).then_inc(c["decay"], 1)

                    all_done(a, i, *(B_ALL if sweep == 0 else C_ALL[0]))
                    a.preload_act_table_set("natural_log_exp_and_others")
                    pipelined(a, NB, [(1, decay), (0, soft)])

                def squares(b, p):
                    a.wait_ge(ready, 1)
                    a.wait_ge(d_yc, done(i, b))
                    a.wait_ge(d_norm, done(i, b - 2))
                    a.activation(halves(tile(p)), pair(2 * p), ACT.Square).then_inc(d_sq, 1)

                def root(b, p):
                    a.wait_ge(ready, 1)
                    a.wait_ge(d_var, done(i, b))
                    a.activation(halves(tile(p)), pair(4), ACT.Ln, bias=col("eps")).then_inc(d_log, 1)
                    a.wait_ge(ready, 1)
                    a.wait_ge(d_log, done(i, b))
                    a.activation(tile(p), tile(p), ACT.Exp, scale=-0.5).then_inc(d_rstd, 1)

                all_done(a, i, *C_ALL[1])
                a.preload_act_table_set("natural_log_exp_and_others")
                pipelined(a, NB, [(1, root), (0, squares)])

                def norm_phase(which, before):
                    n = n_sets[which]

                    def squares(b, p):
                        a.wait_ge(ready, 1)
                        a.wait_ge(n["yc"], done(i, b))
                        a.wait_ge(n["tn"], done(i, b - 2))
                        a.activation(halves(tile(2 + p)), pair(2 + 2 * p), ACT.Square).then_inc(n["sq"], 1)

                    def root(b, p):
                        a.wait_ge(ready, 1)
                        a.wait_ge(n["var"], done(i, b))
                        a.activation(halves(tile(2 + p)), pair(6), ACT.Ln, bias=col("eps")).then_inc(n["log"], 1)
                        a.wait_ge(ready, 1)
                        a.wait_ge(n["log"], done(i, b))
                        a.activation(tile(2 + p), tile(2 + p), ACT.Exp, scale=-0.5).then_inc(n["rstd"], 1)

                    all_done(a, i, *before)
                    a.preload_act_table_set("natural_log_exp_and_others")
                    pipelined(a, NB, [(1, root), (0, squares)])

                norm_phase(0, D_ALL)

                def silu_act(b, p):
                    a.wait_ge(ready, 1)
                    a.wait_ge(e2_mm, done(i, b))
                    a.activation(halves(flat(2, b)), pair(2), ACT.Silu, bias=col("act_o")).then_inc(e2_act, 1)

                def silu_v(b, p):
                    a.wait_ge(ready, 1)
                    a.wait_ge(e2_sum, done(i, b))
                    a.activation(prow(0, b), tile(p).rearrange("p (r w) -> p r w", w=S), ACT.Silu).then_inc(e2_v, 1)

                all_done(a, i, *N_ALL[0])
                pipelined(a, NB, [(0, silu_act), (2, silu_v)])

                def key_exp(b, p):
                    kin = token_psum(p)
                    a.wait_ge(ready, 1)
                    a.wait_ge(f1_min, done(i, b))
                    a.activation(tile(2 + p), tile(2 + p), ACT.Exp).then_inc(f1_exp, 1)
                    a.wait_ge(ready, 1)
                    a.wait_ge(f1_mm, done(i, b))
                    a.wait_ge(f1_kv, done(i, b - 2))
                    a.activation(by_tile(tile(4 + p)), kin[:, :, P:2 * P], ACT.Copy).then_inc(f1_vT, 1)

                all_done(a, i, *E2_ALL)
                a.preload_act_table_set("natural_log_exp_and_others")
                pipelined(a, NB, [(0, key_exp)])

                def query_exp(b, p):
                    a.wait_ge(ready, 1)
                    a.wait_ge(f2_min, done(i, b))
                    a.activation(region_tile(3, 8 + p), region_tile(3, 8 + p), ACT.Exp).then_inc(f2_exp, 1)

                def reciprocal(b, p):
                    a.wait_ge(ready, 1)
                    a.wait_ge(f2_den, done(i, b))
                    a.activation(halves(region_tile(3, 10 + p)), pair(2), ACT.Ln, bias=col("tiny")).then_inc(f2_log, 1)
                    a.wait_ge(ready, 1)
                    a.wait_ge(f2_log, done(i, b))
                    a.activation(region_tile(3, 10 + p), region_tile(3, 10 + p), ACT.Exp, scale=-1.0).then_inc(f2_z, 1)

                all_done(a, i, *F1_ALL)
                a.preload_act_table_set("natural_log_exp_and_others")
                pipelined(a, NB, [(0, query_exp), (1, reciprocal)])

                norm_phase(1, F2_ALL)

                def gelus(b, p):
                    for j in range(4):
                        a.wait_ge(ready, 1)
                        a.wait_ge(g2_fc1, steps(i, b, 4, 4 * CREDIT + j + 1))
                        a.wait_ge(g2_fc2, done(i, b - 2))
                        a.activation(halves(tile(4 * p + j)), pair(2 * (j % 2)), ACT.Gelu, bias=col("fc1_o", j))\
                            .then_inc(g2_gelu, 1)

                def sign(b, p):
                    a.wait_ge(ready, 1)
                    a.wait_ge(g2_x3, done(i, b))
                    a.activation(signs()[:, ds(ROWS * b + 1, ROWS), 1:1 + S],
                                 flat(3, b).rearrange("p (r w) -> p r w", w=S), ACT.Sign).then_inc(g2_sign, 1)

                a.wait_ge(borders, i * 4 + 4)
                all_done(a, i, *N_ALL[1])
                pipelined(a, NB, [(0, gelus), (2, sign)])

                def scale_out(b, p):
                    a.wait_ge(ready, 1)
                    a.wait_ge(h_mm, done(i, b))
                    a.wait_ge(h_store[p], landed(i, b, p))
                    a.activation(halves(tile(p)), pair(2 * p), ACT.Copy, scale=col("w3_s")).then_inc(h_scale, 1)

                all_done(a, i, *G2_ALL)
                pipelined(a, NB, [(0, scale_out)])

        @block.tensor
        def _(pe):
            credit(pe, "p")
            pe.wait_ge(setup_vec, 3)
            pe.wait_ge(setup_loaded, 16 * len(loads))
            pe.wait_ge(late_loaded, 16 * len(late_loads))
            pe.matmul(psum[:, 0, 0:256], cv1, rhs_l1, start=True, stop=True)
            pe.matmul(psum[:, 0, 256:384], opj2, cv2Ts, start=True, stop=True)
            pe.matmul(psum[:, 0, 384:512], ones_row, kb_row, start=True, stop=True)
            for k in range(4):
                pe.matmul(psum[:, 1, P * (k // 2):P * (k // 2) + P], xp_r[:, P * k:P * (k + 1)], dt_r[:, P * k:P * (k + 1)],
                          start=(k % 2 == 0), stop=(k % 2 == 1))
            for k in range(4):
                pe.matmul(psum[:, 2, P * k:P * (k + 1)], bc_r[:, P * k:P * (k + 1)], half_ones, start=True, stop=True)
            pe.matmul(psum[:, 3, 0:1], rhs_l1[:, 0:P], col("l1_cv1b", rows=slice(0, CM)), start=True, stop=True)
            pe.matmul(psum[:, 3, 1:2], rhs_l1[:, P:2 * P], col("l1_cv1b", rows=slice(0, CM)), start=True, stop=True)
            pe.matmul(psum[:, 3, 2:3], raw_in, col("n1_b"), start=True, stop=True)
            pe.matmul(psum[:, 3, 3:4], raw_act, col("n1_b"), start=True, stop=True)
            for j in range(4):
                last = pe.matmul(psum[:, 3, 4 + j:5 + j], raw_fc1[:, P * j:P * (j + 1)], col("n2_b"), start=True, stop=True)
            last.then_inc(setup_pe, 1)
            pe.wait_ge(ready, 1)

            def product(bank, terms):
                for s in range(2):
                    for n, (weights, moving) in enumerate(terms):
                        last = pe.matmul(psum[:, bank + s, 0:HC], weights[:, :], moving(s),
                                         start=(n == 0), stop=(n == len(terms) - 1))
                return last

            def flat_rows(k, b):
                return lambda s: R[k][:, ds(BLK * b + HC * s, HC)]

            def image_rows(k, b, dh=0, dw=0):
                return lambda s: prow(k, b, dh, dw, rows=HALF, skip=HALF * s)

            def static(ap):
                return lambda s: ap[:, HC * s:HC * (s + 1)]

            def taps(conv, k, b):
                return [(d, image_rows(k, b, *tap)) for d, tap in zip(diag[conv], TAPS[VECTOR_TAPS[conv]:])]

            with pe.Fori(0, B, 1) as i:
                def l0(b, p):
                    pe.wait_ge(ready, 1)
                    pe.wait_ge(l0_high, done(i, b))
                    pe.wait_ge(l0_relu, done(i, b - 2))
                    product(2 * p, [(ph_a, lambda s: high[p][:, 1 + HALF * s:1 + HALF * (s + 1), :]),
                                    (ph_b, lambda s: high[p][:, HALF * s:HALF * (s + 1), :])])
                    pe.matmul(psum[:, 4 + p, 0:QUARTER], magT[:, :], low_wide[p][:, 0::2], start=True, stop=True)\
                        .then_inc(l0_mm, 1)

                pipelined(pe, NB, [(0, l0)])

                def xz(b, p):
                    pe.wait_ge(ready, 1)
                    pe.wait_ge(a_xc, done(i, b - 2))
                    pe.wait_ge(a_act, done(i, b - 2))
                    product(2 * p, [(w_xc, image_rows(0, b))])
                    product(4 + 2 * p, [(w_z, image_rows(0, b))]).then_inc(a_mm, 1)

                all_done(pe, i, *L0_ALL)
                pipelined(pe, NB, [(0, xz)])

                def l1_conv(b, p):
                    pe.wait_ge(ready, 1)
                    pe.wait_ge(b_act, done(i, b - 2))
                    both = [(dwl1[n], image_rows(3, b, -1, n - 1)) for n in range(3)]
                    lower = [(dwl1[3 + n][0:CM], (lambda m: lambda s: m(s)[0:CM])(image_rows(3, b, 1, n - 1)))
                             for n in range(3)]
                    product(2 * p, both + lower).then_inc(b_mm, 1)

                all_done(pe, i, *A_ALL)
                pipelined(pe, NB, [(0, l1_conv)])

                for sweep in range(2):
                    c = c_sets[sweep]

                    def dt(b, p):
                        pe.wait_ge(ready, 1)
                        pe.wait_ge(c["step"], done(i, b - 2))
                        product(2 * p, [(w_dt[sweep], flat_rows(2, sweep_block(sweep, b)))]).then_inc(c["dt"], 1)

                    def bc(b, p):
                        pe.wait_ge(ready, 1)
                        pe.wait_ge(c["bu"], done(i, b - 1))
                        product(4, [(w_B[sweep], flat_rows(2, sweep_block(sweep, b)))]).then_inc(c["B"], 1)
                        pe.wait_ge(ready, 1)
                        pe.wait_ge(c["hc"], done(i, b - 1))
                        product(6, [(w_C[sweep], flat_rows(2, sweep_block(sweep, b)))]).then_inc(c["C"], 1)

                    all_done(pe, i, *(B_ALL if sweep == 0 else C_ALL[0]))
                    pipelined(pe, NB, [(0, dt), (1, bc)])

                def yc(b, p):
                    pe.wait_ge(ready, 1)
                    pe.wait_ge(d_norm, done(i, b - 2))
                    cols_of = R[3][:, 0:N].rearrange("p (w h) -> p h w", h=S)
                    product(2 * p, [(cen64[0:CM], lambda s: R[3][0:CM, ds(BLK * b + HC * s, HC)]),
                                    (cen64_d[0:CM], lambda s: R[2][0:CM, ds(BLK * b + HC * s, HC)]),
                                    (cen64_up, lambda s: cols_of[:, ds(ROWS * b + HALF * s, HALF), :])])\
                        .then_inc(d_yc, 1)

                def var(b, p):
                    pe.wait_ge(ready, 1)
                    pe.wait_ge(d_sq, done(i, b))
                    pe.wait_ge(d_log, done(i, b - 1))
                    product(4, [(avg128, static(tile(p)))]).then_inc(d_var, 1)

                def l1_out(b, p):
                    pe.wait_ge(ready, 1)
                    pe.wait_ge(d_gate, done(i, b))
                    pe.wait_ge(d_out, done(i, b - 1))
                    product(6, [(w_l1out, flat_rows(1, b))]).then_inc(d_mm, 1)

                all_done(pe, i, *C_ALL[1])
                pipelined(pe, NB, [(3, l1_out), (1, var), (0, yc)])

                def norm_phase(which, conv, source, centre_from, before):
                    n = n_sets[which]

                    def convolve(b, p):
                        pe.wait_ge(ready, 1)
                        pe.wait_ge(n["t"], done(i, b - 1))
                        product(0, taps(conv, source, b)).then_inc(n["conv"], 1)

                    def centre(b, p):
                        pe.wait_ge(ready, 1)
                        pe.wait_ge(n["t"], done(i, b))
                        pe.wait_ge(n["tn"], done(i, b - 2))
                        product(2 + 2 * p, [(cen128, centre_from(b))]).then_inc(n["yc"], 1)

                    def var(b, p):
                        pe.wait_ge(ready, 1)
                        pe.wait_ge(n["sq"], done(i, b))
                        pe.wait_ge(n["log"], done(i, b - 1))
                        product(6, [(avg128, static(tile(2 + p)))]).then_inc(n["var"], 1)

                    all_done(pe, i, *before)
                    pipelined(pe, NB, [(2, var), (1, centre), (0, convolve)])

                norm_phase(0, "cpe1", 0, lambda b: image_rows(1, b), D_ALL)

                def in_act(b, p):
                    pe.wait_ge(ready, 1)
                    pe.wait_ge(e2_ti, done(i, b - 1))
                    pe.wait_ge(e2_act, done(i, b - 1))
                    product(0, [(w_in, flat_rows(2, b))])
                    product(2, [(w_act, flat_rows(2, b))]).then_inc(e2_mm, 1)

                def dwc(b, p):
                    pe.wait_ge(ready, 1)
                    pe.wait_ge(e2_ti, done(i, b if isinstance(b, int) and b == NB - 1 else b + 1))
                    pe.wait_ge(e2_sum, done(i, b - 2))
                    product(4 + 2 * p, taps("dwc", 3, b)).then_inc(e2_conv, 1)

                all_done(pe, i, *N_ALL[0])
                pipelined(pe, NB, [(0, in_act), (2, dwc)])

                def keys(b, p):
                    kin = token_psum(p)
                    pe.wait_ge(ready, 1)
                    pe.wait_ge(f1_stage, done(i, b))
                    pe.wait_ge(f1_bias, done(i, b - 2))
                    pe.wait_ge(f1_vT, done(i, b - 2))
                    for n in range(NT):
                        last = pe.matmul(kin[:, n, :], region_tile(3, p)[:, P * n:P * (n + 1)], w_ki[:, :],
                                         start=True, stop=True)
                    last.then_inc(f1_mm, 1)

                def kv_sum(b, p):
                    pe.wait_ge(ready, 1)
                    pe.wait_ge(f1_vT, done(i, b))
                    pe.wait_ge(f1_kc, done(i, b))
                    pe.wait_ge(f1_ks, done(i, b))
                    for n in range(NT):
                        first = isinstance(b, int) and b == 0 and n == 0
                        final = isinstance(b, int) and b == NB - 1 and n == NT - 1
                        last = pe.matmul(psum[:, 6, 0:2 * P], tile(4 + p)[:, P * n:P * (n + 1)], kcs(p)[:, n, :],
                                         start=first, stop=final)
                    last.then_inc(f1_kv, 1)

                all_done(pe, i, *E2_ALL)
                pipelined(pe, NB, [(0, keys), (2, kv_sum)])

                acc = region_tile(3, 8)
                turned = region_tile(3, 9)
                pe.wait_ge(ready, 1)
                pe.wait_ge(kv_vec, i * 4 + 1)
                pe.wait_ge(f1_ksum, done(i, NB - 1))
                pe.matmul(psum[:, 7, 0:P], acc[:, 0:P], ident[:, :], start=True, stop=True)
                pe.matmul(psum[:, 7, P:2 * P], acc[:, P:2 * P], ident[:, :], start=True, stop=True)
                for n in range(NT):
                    last = pe.matmul(psum[:, 6, 300:301], tile(6)[:, P * n:P * (n + 1)], col("one"),
                                     start=(n == 0), stop=(n == NT - 1))
                last.then_inc(kv_pe, 1)
                pe.wait_ge(ready, 1)
                pe.wait_ge(kv_vec, i * 4 + 2)
                pe.matmul(psum[:, 0, 0:P], ident[:, :], turned[:, 0:P], start=True, stop=False)
                pe.matmul(psum[:, 0, 0:P], rotT[:, :], turned[:, P:2 * P], start=False, stop=True).then_inc(kv_pe, 1)
                pe.wait_ge(ready, 1)
                pe.wait_ge(kv_vec, i * 4 + 3)
                pe.matmul(psum[:, 1, 0:P], rot[:, :], kv[:, :], start=True, stop=True).then_inc(kv_pe, 1)
                pe.wait_ge(kv_vec, i * 4 + 4)

                def query(b, p):
                    pe.wait_ge(ready, 1)
                    pe.wait_ge(f2_phi, done(i, b - 1))
                    product(0, [(w_q, image_rows(0, b))]).then_inc(f2_q, 1)
                    pe.wait_ge(ready, 1)
                    pe.wait_ge(f2_lepe, done(i, b - 1))
                    product(6, taps("lepe", 0, b)).then_inc(f2_conv, 1)

                def attend(b, p):
                    pe.wait_ge(ready, 1)
                    pe.wait_ge(f2_phi, done(i, b))
                    pe.wait_ge(f2_t2, done(i, b - 1))
                    product(2, [(kmean, static(tile(p)))]).then_inc(f2_den, 1)
                    pe.wait_ge(ready, 1)
                    pe.wait_ge(f2_qc, done(i, b))
                    pe.wait_ge(f2_qs, done(i, b))
                    pe.wait_ge(f2_nz, done(i, b - 1))
                    product(4, [(kv, static(region_tile(3, 4 + p))), (kv_rot, static(region_tile(3, 6 + p)))])\
                        .then_inc(f2_num, 1)

                def project(b, p):
                    pe.wait_ge(ready, 1)
                    pe.wait_ge(f2_ta, done(i, b))
                    pe.wait_ge(f2_log, done(i, b))
                    product(2, [(w_out, static(tile(4 + p)))]).then_inc(f2_out, 1)

                all_done(pe, i, *F1_ALL)
                pipelined(pe, NB, [(2, project), (1, attend), (0, query)])

                norm_phase(1, "cpe2", 1, lambda b: flat_rows(3, b), F2_ALL)

                def mlp_up(b, p):
                    for j in range(4):
                        pe.wait_ge(ready, 1)
                        pe.wait_ge(g2_gelu, steps(i, b, 4, 4 * CREDIT + j - 1))
                        product(2 * (j % 2), [(fc1[:, P * j:P * (j + 1)], flat_rows(2, b))]).then_inc(g2_fc1, 1)

                def mlp_down(b, p):
                    pe.wait_ge(ready, 1)
                    pe.wait_ge(g2_gelu, steps(i, b, 4, 4 * CREDIT + 4))
                    pe.wait_ge(g2_x3, done(i, b - 2))
                    product(4 + 2 * p, [(fc2[:, P * j:P * (j + 1)], static(tile(4 * p + j))) for j in range(4)])\
                        .then_inc(g2_fc2, 1)

                all_done(pe, i, *N_ALL[1])
                pipelined(pe, NB, [(0, mlp_up), (1, mlp_down)])

                def l3(b, p):
                    pe.wait_ge(ready, 1)
                    pe.wait_ge(h_scale, done(i, b - 2))
                    for s in range(2):
                        for n, (dh, dw) in enumerate(TAPS):
                            k = tap_column((dh, dw))
                            last = pe.matmul(psum[:, 2 * p + s, 0:HC], w3[:, P * k:P * (k + 1)],
                                             signs()[:, ds(ROWS * b + (1 + dh + HALF * s), HALF), 1 + dw:1 + dw + S],
                                             start=(n == 0), stop=(n == 8))
                    last.then_inc(h_mm, 1)

                all_done(pe, i, *G2_ALL)
                pipelined(pe, NB, [(0, l3)])
                all_done(pe, i, *H_ALL)

        @block.vector
        def _(v):
            credit(v, "v")
            count = [0]

            def link(ins):
                count[0] += 1
                ins.then_inc(setup_steps, 1)
                v.wait_ge(setup_steps, count[0])

            v.memset(xp_r, 0.0)
            v.memset(dt_r, 0.0)
            link(v.memset(bc_r, 0.0))
            v.memset(ones_row, 1.0).then_inc(setup_vec, 1)
            v.wait_ge(setup_loaded, 16 * len(loads))
            v.memset(col("zero"), 0.0)
            v.memset(col("one"), 1.0)
            v.memset(col("tiny"), 1e-6)
            link(v.memset(col("eps"), EPS))
            v.memset(col("ksum"), 0.0).then_inc(setup_vec, 1)
            link(v.tensor_scalar(cv2Ts, cv2T, col("l1_scale", rows=slice(0, CM)), None, ALU.mult))
            v.memset(col("ksum"), 0.0).then_inc(setup_vec, 1)
            v.wait_ge(setup_act, 1)
            for name, root_name in (("mag", "root"), ("ph", "root2")):
                link(v.reciprocal(col(root_name), col(root_name)))
                link(v.tensor_tensor(col(name + "_s"), col(name + "_gamma"), col(root_name), ALU.mult))
                link(v.tensor_tensor(col(name + "_o"), col(name + "_b"), col(name + "_mean"), ALU.subtract))
                link(v.tensor_tensor(col(name + "_o"), col(name + "_o"), col(name + "_s"), ALU.mult))
                link(v.tensor_tensor(col(name + "_o"), col(name + "_o"), col(name + "_beta"), ALU.add))
                link(v.tensor_scalar(col(name + "_ns"), col(name + "_s"), -1.0, None, ALU.mult))
                link(v.tensor_scalar(col(name + "_no"), col(name + "_o"), -1.0, None, ALU.mult))
            v.tensor_scalar(col("nalpha"), col("alpha"), -1.0, None, ALU.mult)
            for n in range(2):
                v.tensor_scalar(col(f"l1_A{n}"), col(f"l1_A{n}"), -1.0, None, ALU.mult)
            v.tensor_scalar(col("w3_s"), col("w3_s"), 1.0 / (9 * P), None, ALU.mult)
            v.tensor_scalar(col("q_b1"), col("q_b"), 1.0, None, ALU.add)
            for conv in ("cpe1", "cpe2"):
                v.tensor_scalar(tap_weight(conv, (0, 0)), tap_weight(conv, (0, 0)), 1.0, None, ALU.add)
            link(v.reduce_sum(col("Dsum"), cols[:, at["l1_D"]:at["l1_D"] + 4], mybir.AxisListType.X))
            v.tensor_scalar(cen64_d[:, :], cen64[:, :], col("Dsum"), None, ALU.mult)
            for conv in convs:
                for d, tap in zip(diag[conv], TAPS[VECTOR_TAPS[conv]:]):
                    v.tensor_scalar(d[:, :], ident[:, :], tap_weight(conv, tap), None, ALU.mult)
            for n in range(6):
                v.tensor_scalar(dwl1[n][:, :], e2mask, col("l1taps", n), None, ALU.mult)
            v.tensor_scalar(w_in[:, :], raw_in, col("n1_g"), None, ALU.mult)
            v.tensor_scalar(w_act[:, :], raw_act, col("n1_g"), None, ALU.mult)
            v.tensor_scalar(fc1[:, :], raw_fc1, col("n2_g"), None, ALU.mult)
            v.wait_ge(setup_pe, 1)
            v.tensor_copy(w_xc[:, :], psum[:, 0, 0:128])
            v.tensor_copy(w_z[:, :], psum[:, 0, 128:256])
            v.tensor_scalar(w_l1out[:, :], psum[:, 0, 256:384], col("l1_gb"), None, ALU.mult)
            v.tensor_copy(kbias[:, :], psum[:, 0, 384:512])
            for n in range(2):
                v.tensor_copy(w_dt[n][:, :], psum[:, 1, P * n:P * (n + 1)])
                v.tensor_copy(w_B[n][:, :], psum[:, 2, 2 * P * n:2 * P * n + P])
                v.tensor_copy(w_C[n][:, :], psum[:, 2, 2 * P * n + P:2 * P * (n + 1)])
            v.tensor_copy(col("xc_b"), psum[:, 3, 0:1])
            v.tensor_copy(col("z_b"), psum[:, 3, 1:2])
            v.tensor_tensor(col("in_o"), psum[:, 3, 2:3], col("in_b"), ALU.add)
            v.tensor_tensor(col("act_o"), psum[:, 3, 3:4], col("act_b"), ALU.add)
            v.tensor_tensor(cols[:, at["fc1_o"]:at["fc1_o"] + 4], psum[:, 3, 4:8], cols[:, at["fc1_b"]:at["fc1_b"] + 4], ALU.add)
            link(v.memset(R[0][:, :], 0.0))
            v.sem_inc(ready, 1)

            def vector_taps(i, conv, k, b, target, bias):
                mine = TAPS[:VECTOR_TAPS[conv]]
                each = len(mine)
                tgt = target.rearrange("p (r w) -> p r w", w=S)
                for n, tap in enumerate(mine):
                    if n:
                        v.wait_ge(ready, 1)
                        v.wait_ge(tap_steps[conv], steps(i, b, each, n))
                        v.scalar_tensor_tensor(out=tgt, in0=prow(k, b, *tap), scalar=tap_weight(conv, tap), in1=tgt,
                                               op0=ALU.mult, op1=ALU.add).then_inc(tap_steps[conv], 1)
                    else:
                        v.tensor_scalar(tgt, prow(k, b, *tap), tap_weight(conv, tap), bias, ALU.mult, ALU.add)\
                            .then_inc(tap_steps[conv], 1)
                v.wait_ge(tap_steps[conv], steps(i, b, each, each))

            with v.Fori(0, B, 1) as i:
                def split(b, p):
                    xr = x_tile[p].rearrange("p (r w) -> p r w", w=S)
                    pairs = pair_sum[p].rearrange("p (r w) -> p r w", w=S // 2)
                    quads = quad_sum[p].rearrange("p (r w) -> p r w", w=S // 2)
                    wide = low_wide[p].rearrange("p (r w e) -> p r w e", w=S // 2, e=2)
                    wrows = low_wide[p].rearrange("p (r w) -> p r w", w=S)
                    v.wait_ge(ready, 1)
                    v.wait_ge(x_in[p], landed(i, b, p))
                    v.tensor_tensor(pairs, xr[:, :, 0::2], xr[:, :, 1::2], ALU.add).then_inc(l0_steps, 1)
                    v.wait_ge(ready, 1)
                    v.wait_ge(l0_steps, steps(i, b, 3, 1))
                    v.tensor_tensor(quads, pairs[:, 0::2, :], pairs[:, 1::2, :], ALU.add).then_inc(l0_steps, 1)
                    v.wait_ge(ready, 1)
                    v.wait_ge(l0_steps, steps(i, b, 3, 2))
                    v.wait_ge(l0_mm, done(i, b - 2))
                    v.tensor_scalar(wide, quads.unsqueeze(3).broadcast_to((P, HALF, S // 2, 2)), 0.25, None, ALU.mult)\
                        .then_inc(l0_steps, 1)
                    v.wait_ge(ready, 1)
                    v.wait_ge(l0_steps, steps(i, b, 3, 3))
                    v.tensor_tensor(high[p][:, 1:1 + ROWS, :].rearrange("p (r e) w -> p r e w", e=2),
                                    xr.rearrange("p (r e) w -> p r e w", e=2),
                                    wrows.unsqueeze(2).broadcast_to((P, HALF, 2, S)), ALU.subtract)
                    v.tensor_tensor(high[p][:, 0, :], xr[:, ROWS - 1, :], wrows[:, HALF - 1, :], ALU.subtract)\
                        .then_inc(l0_high, 1)

                def join(b, p):
                    lows = low_pos[p].rearrange("p (r w) -> p r w", w=S // 2)
                    v.wait_ge(ready, 1)
                    v.wait_ge(l0_relu, done(i, b))
                    v.scalar_tensor_tensor(out=low_pos[p], in0=low_neg[p], scalar=col("nalpha"), in1=low_pos[p],
                                           op0=ALU.mult, op1=ALU.add).then_inc(l0_join, 1)
                    v.scalar_tensor_tensor(out=hs_pos[p], in0=hs_neg[p], scalar=col("nalpha"), in1=hs_pos[p],
                                           op0=ALU.mult, op1=ALU.add).then_inc(l0_join, 1)
                    v.wait_ge(ready, 1)
                    v.wait_ge(l0_join, steps(i, b, 3, 1))
                    v.tensor_copy(out_low.rearrange("p (r w e) -> p r w e", w=S // 2, e=2),
                                  lows.unsqueeze(3).broadcast_to((P, HALF, S // 2, 2))).then_inc(l0_join, 1)
                    v.wait_ge(ready, 1)
                    v.wait_ge(l0_join, steps(i, b, 3, 3))
                    v.tensor_tensor(prow(0, b).rearrange("p (r e) w -> p r e w", e=2),
                                    hs_pos[p].rearrange("p (r e w) -> p r e w", e=2, w=S),
                                    out_low.rearrange("p (r w) -> p r w", w=S).unsqueeze(2).broadcast_to((P, HALF, 2, S)),
                                    ALU.add).then_inc(l0_out, 1)

                all_done(v, i - 1, *G2_ALL)
                pipelined(v, NB, [(0, split), (2, join)])

                def xc(b, p):
                    v.wait_ge(ready, 1)
                    v.wait_ge(a_mm, done(i, b))
                    v.tensor_scalar(pad_rows(3, b, slice(0, CM)), rows_of(pair(2 * p))[0:CM],
                                    col("xc_b", rows=slice(0, CM)), None, ALU.add).then_inc(a_xc, 1)

                v.wait_ge(borders, i * 4 + 1)
                all_done(v, i, *L0_ALL)
                pipelined(v, NB, [(0, xc)])

                for p in range(2):
                    v.wait_ge(h_store[p], i * (8 * NB) + 16)
                for sweep in range(2):
                    c = c_sets[sweep]
                    edge = BLK - 1 if sweep == 0 else 0

                    def cap(b, p):
                        v.wait_ge(ready, 1)
                        v.wait_ge(c["dt"], done(i, b))
                        v.wait_ge(c["decay"], done(i, b - 2))
                        v.wait_ge(c["du"], done(i, b - 2))
                        v.tensor_scalar(halves(tile(p)), pair(2 * p), col(f"l1_dtb{sweep}"), CAP, ALU.add, ALU.min)\
                            .then_inc(c["cap"], 1)

                    def step_size(b, p):
                        v.wait_ge(ready, 1)
                        v.wait_ge(c["log"], done(i, b))
                        v.scalar_tensor_tensor(out=halves(tile(p)), in0=pair(2 * p), scalar=col(f"l1_dtb{sweep}"),
                                               in1=halves(tile(p)), op0=ALU.add, op1=ALU.max).then_inc(c["step"], 1)

                    def scan(b, p):
                        v.wait_ge(ready, 1)
                        v.wait_ge(c["du"], done(i, b))
                        v.wait_ge(c["B"], done(i, b))
                        v.tensor_tensor(halves(tile(2 + p)), halves(tile(2 + p)), pair(4), ALU.mult).then_inc(c["bu"], 1)
                        v.wait_ge(ready, 1)
                        v.wait_ge(c["bu"], done(i, b))
                        v.wait_ge(c["decay"], done(i, b))
                        first = isinstance(b, int) and b == 0
                        start = col("zero") if first else tile(7 - p)[:, edge:edge + 1]
                        way = (lambda ap: ap) if sweep == 0 else (lambda ap: ap[:, ::-1])
                        v.tensor_tensor_scan(way(tile(6 + p)), way(tile(4 + p)), way(tile(2 + p)), initial=start,
                                             op0=ALU.mult, op1=ALU.add).then_inc(c["h"], 1)

                    def outputs(b, p):
                        v.wait_ge(ready, 1)
                        v.wait_ge(c["h"], done(i, b))
                        v.wait_ge(c["C"], done(i, b))
                        y = flat(3, b) if sweep == 0 else tile(4 + p)
                        v.tensor_tensor(halves(y), halves(tile(6 + p)), pair(6), ALU.mult).then_inc(c["hc"], 1)

                    all_done(v, i, *(B_ALL if sweep == 0 else C_ALL[0]))
                    pipelined(v, NB, [(0, cap), (2, scan), (1, step_size), (2, outputs)])

                def normalise(b, p):
                    v.wait_ge(ready, 1)
                    v.wait_ge(d_rstd, done(i, b))
                    v.wait_ge(d_gate, done(i, b - 2))
                    v.tensor_tensor(halves(tile(2 + p)), halves(tile(p)), pair(2 * p), ALU.mult).then_inc(d_norm, 1)

                def residual(b, p):
                    v.wait_ge(ready, 1)
                    v.wait_ge(d_mm, done(i, b))
                    for s in range(2):
                        x = prow(0, b, rows=HALF, skip=HALF * s)
                        last = v.scalar_tensor_tensor(out=x, in0=pair(6)[:, s].rearrange("p (r w) -> p r w", w=S),
                                                      scalar=col("cv2_b"), in1=x, op0=ALU.add, op1=ALU.add)
                    last.then_inc(d_out, 1)

                all_done(v, i, *C_ALL[1])
                pipelined(v, NB, [(3, residual), (1, normalise)])

                def norm_phase(which, conv, source, target_of, before):
                    n = n_sets[which]

                    def convolve(b, p):
                        v.wait_ge(ready, 1)
                        v.wait_ge(n["t"], done(i, b - 2))
                        vector_taps(i, conv, source, b, tile(p), col(conv + "_b"))
                        v.wait_ge(ready, 1)
                        v.wait_ge(n["conv"], done(i, b))
                        v.tensor_tensor(target_of(b), by_rows(tile(p)), rows_of(pair(0)), ALU.add).then_inc(n["t"], 1)

                    def normalise(b, p):
                        v.wait_ge(ready, 1)
                        v.wait_ge(n["rstd"], done(i, b))
                        v.tensor_tensor(halves(flat(2, b)), halves(tile(2 + p)), pair(2 + 2 * p), ALU.mult)\
                            .then_inc(n["tn"], 1)

                    all_done(v, i, *before)
                    pipelined(v, NB, [(3, normalise), (0, convolve)])

                v.wait_ge(borders, i * 4 + 3)
                norm_phase(0, "cpe1", 0, lambda b: prow(1, b).rearrange("p (a r) w -> p a r w", a=2), D_ALL)

                def ti(b, p):
                    v.wait_ge(ready, 1)
                    v.wait_ge(e2_mm, done(i, b))
                    v.tensor_scalar(prow(3, b).rearrange("p (a r) w -> p a r w", a=2), rows_of(pair(0)), col("in_o"),
                                    None, ALU.add).then_inc(e2_ti, 1)

                def dwc(b, p):
                    v.wait_ge(ready, 1)
                    v.wait_ge(e2_ti, done(i, b if isinstance(b, int) and b == NB - 1 else b + 1))
                    v.wait_ge(e2_v, done(i, b - 2))
                    vector_taps(i, "dwc", 3, b, tile(p), col("dwc_b"))
                    v.wait_ge(ready, 1)
                    v.wait_ge(e2_conv, done(i, b))
                    v.tensor_tensor(halves(tile(p)), halves(tile(p)), pair(4 + 2 * p), ALU.add).then_inc(e2_sum, 1)

                all_done(v, i, *N_ALL[0])
                pipelined(v, NB, [(2, dwc), (0, ti)])

                def key_in(b, p):
                    v.wait_ge(ready, 1)
                    v.wait_ge(f1_mm, done(i, b))
                    v.wait_ge(f1_kc, done(i, b - 2))
                    v.wait_ge(f1_ksum, done(i, b - 2))
                    v.wait_ge(f1_ks, done(i, b - 2))
                    v.tensor_tensor(by_tile(tile(p)), token_psum(p)[:, :, 0:P],
                                    kbias[:, :].unsqueeze(1).broadcast_to((P, NT, P)), ALU.add).then_inc(f1_bias, 1)
                    v.wait_ge(ready, 1)
                    v.wait_ge(f1_bias, done(i, b))
                    v.tensor_scalar(tile(2 + p), tile(p), 0.0, None, ALU.min).then_inc(f1_min, 1)

                def key_out(b, p):
                    v.wait_ge(ready, 1)
                    v.wait_ge(f1_exp, done(i, b))
                    v.scalar_tensor_tensor(out=tile(p), in0=tile(p), scalar=1.0, in1=tile(2 + p), op0=ALU.add,
                                           op1=ALU.max).then_inc(f1_k, 1)
                    v.wait_ge(ready, 1)
                    v.wait_ge(f1_k, done(i, b))
                    v.wait_ge(f1_tab[p], landed(i, b, p))
                    v.wait_ge(f1_kv, done(i, b - 2))
                    v.tensor_tensor(by_pairs(kcs(p)[:, :, P:2 * P]), by_pairs(by_tile(tile(p))), tok_table(p, 1), ALU.mult)\
                        .then_inc(f1_ks, 1)

                all_done(v, i, *E2_ALL)
                pipelined(v, NB, [(0, key_in), (1, key_out)])

                all_done(v, i, *F1_ALL)
                v.tensor_copy(region_tile(3, 8)[:, 0:2 * P], psum[:, 6, 0:2 * P]).then_inc(kv_vec, 1)
                v.wait_ge(ready, 1)
                v.wait_ge(kv_pe, i * 3 + 1)
                v.tensor_copy(region_tile(3, 9)[:, 0:2 * P], psum[:, 7, 0:2 * P])
                v.tensor_scalar(kmean[:, :], headmask[:, :], psum[:, 6, 300:301], 1.0 / N, ALU.mult, ALU.mult)\
                    .then_inc(kv_vec, 1)
                v.wait_ge(ready, 1)
                v.wait_ge(kv_pe, i * 3 + 2)
                v.scalar_tensor_tensor(out=kv[:, :], in0=psum[:, 0, 0:P], scalar=1.0 / N, in1=headmask[:, :],
                                       op0=ALU.mult, op1=ALU.mult).then_inc(kv_vec, 1)
                v.wait_ge(ready, 1)
                v.wait_ge(kv_pe, i * 3 + 3)
                v.tensor_copy(kv_rot[:, :], psum[:, 1, 0:P]).then_inc(kv_vec, 1)

                def query_in(b, p):
                    v.wait_ge(ready, 1)
                    v.wait_ge(f2_q, done(i, b))
                    v.tensor_scalar(halves(region_tile(3, 8 + p)), pair(0), col("q_b"), 0.0, ALU.add, ALU.min)\
                        .then_inc(f2_min, 1)
                    v.wait_ge(ready, 1)
                    v.wait_ge(f2_ta, done(i, b - 2))
                    v.wait_ge(f2_out, done(i, b - 2))
                    vector_taps(i, "lepe", 0, b, tile(4 + p), col("lepe_b"))
                    v.wait_ge(ready, 1)
                    v.wait_ge(f2_conv, done(i, b))
                    v.tensor_tensor(halves(tile(4 + p)), halves(tile(4 + p)), pair(6), ALU.add).then_inc(f2_lepe, 1)
                    v.wait_ge(ready, 1)
                    v.wait_ge(f2_exp, done(i, b))
                    v.wait_ge(f2_den, done(i, b - 2))
                    v.wait_ge(f2_qc, done(i, b - 2))
                    v.scalar_tensor_tensor(out=halves(tile(p)), in0=pair(0), scalar=col("q_b1"),
                                           in1=halves(region_tile(3, 8 + p)), op0=ALU.add, op1=ALU.max).then_inc(f2_phi, 1)
                    v.wait_ge(ready, 1)
                    v.wait_ge(f2_phi, done(i, b))
                    v.wait_ge(f2_tab[p], landed(i, b, p))
                    v.wait_ge(f2_num, done(i, b - 2))
                    v.tensor_tensor(region_tile(3, 6 + p), tile(p), region_tile(3, 2 * p + 1), ALU.mult).then_inc(f2_qs, 1)

                def attention(b, p):
                    v.wait_ge(ready, 1)
                    v.wait_ge(f2_num, done(i, b))
                    v.wait_ge(f2_z, done(i, b))
                    v.wait_ge(f2_sum, done(i, b - 2))
                    v.tensor_tensor(halves(tile(2 + p)), halves(region_tile(3, 10 + p)), pair(4), ALU.mult)\
                        .then_inc(f2_nz, 1)

                def residual2(b, p):
                    v.wait_ge(ready, 1)
                    v.wait_ge(f2_out, done(i, b))
                    for s in range(2):
                        x = prow(1, b, rows=HALF, skip=HALF * s)
                        last = v.scalar_tensor_tensor(out=x, in0=pair(2)[:, s].rearrange("p (r w) -> p r w", w=S),
                                                      scalar=col("out_b"), in1=x, op0=ALU.add, op1=ALU.add)
                    last.then_inc(f2_t2, 1)

                pipelined(v, NB, [(2, residual2), (0, query_in), (1, attention)])

                norm_phase(1, "cpe2", 1, lambda b: by_rows(flat(3, b)), F2_ALL)

                def x3(b, p):
                    v.wait_ge(ready, 1)
                    v.wait_ge(g2_fc2, done(i, b))
                    v.scalar_tensor_tensor(out=halves(flat(3, b)), in0=pair(4 + 2 * p), scalar=col("fc2_b"),
                                           in1=halves(flat(3, b)), op0=ALU.add, op1=ALU.add).then_inc(g2_x3, 1)

                all_done(v, i, *N_ALL[1])
                pipelined(v, NB, [(0, x3)])




def constants(S):
    f = np.float32
    c, d = np.arange(P)[:, None], np.arange(P)[None, :]
    eye = (c == d).astype(f)
    same_half = (c % CM == d % CM).astype(f)
    cen64 = same_half - f(1 / CM)
    up = cen64.copy()
    up[:CM] = 0
    rot = np.zeros((P, P), f)
    rot[0::2, 1::2][np.arange(P // 2), np.arange(P // 2)] = -1
    rot[1::2, 0::2][np.arange(P // 2), np.arange(P // 2)] = 1
    half = np.zeros((2, P), f)
    half[0, :CM], half[1, CM:] = 1, 1
    out = {"c_ident": eye, "c_cen128": eye - f(1 / P), "c_avg128": np.full((P, P), 1 / P, f),
           "c_headmask": (c // (P // HEADS) == d // (P // HEADS)).astype(f), "c_rot": rot, "c_rotT": rot.T.copy(),
           "c_cen64": cen64, "c_cen64_up": up, "c_e2": same_half, "c_half": half}
    k = P // 4
    theta = f(1) / (f(10000.0) ** (np.arange(k, dtype=f) / f(k))).astype(f)
    at = (np.arange(S, dtype=f)[:, None] * theta).astype(f)
    ang = np.concatenate([np.broadcast_to(at[:, None, :], (S, S, k)), np.broadcast_to(at[None, :, :], (S, S, k))], -1)
    nb, blk = S // ROWS, ROWS * S
    ang = ang.reshape(nb, blk, 2 * k)
    cs = np.stack([np.cos(ang), np.sin(ang)]).astype(f)
    tok = cs.reshape(2, nb, blk // P, P, 2 * k).transpose(1, 3, 0, 2, 4).reshape(nb, P, blk)
    ch = np.repeat(cs, 2, axis=3).transpose(1, 3, 0, 2).reshape(nb, P, 2 * blk)
    out["tab_tok"], out["tab_ch"] = np.ascontiguousarray(tok), np.ascontiguousarray(ch)
    return out


def layout(x):
    g = {k: np.asarray(v) for k, v in x.items()}
    l0 = {k[8:]: v for k, v in g.items() if k.startswith("L0_conv_")}
    l1 = {k[8:]: v for k, v in g.items() if k.startswith("L1_conv_")}
    l2 = {k[8:]: v for k, v in g.items() if k.startswith("L2_conv_")}
    w3 = g["L3_conv_weight"]
    a = constants(g["x"].shape[-1])
    a["x"] = g["x"]
    a["ph_aT"], a["ph_bT"] = l0["phase_w"][:P, :P].T, l0["phase_w"][:P, P:].T
    a["magT"] = l0["mag_w"].T
    a["inprojT"], a["cv1_w"], a["out_proj"] = l1["in_proj_w"].T, l1["cv1_w"], l1["out_proj_w"]
    a["cv2T"], a["x_proj"], a["dt_wT"] = l1["cv2_w"].T, l1["x_proj_w"], l1["dt_w"].transpose(0, 2, 1)
    for name in ("inproj_w", "actproj_w", "fc1_w", "fc2_w", "qk_w", "outproj_w"):
        a[name] = l2[name]
    a["kb_row"] = l2["qk_b"][None, P:]
    a["w3_nat"] = w3.reshape(P, 9 * P)
    a["w3_T"] = w3.transpose(1, 2, 3, 0).reshape(P, 9 * P)

    def twice(v):
        return np.concatenate([v, v])

    A, Ds, cw = l1["A_logs"].reshape(4, CM), l1["Ds"].reshape(4, CM), l1["conv_w"].reshape(CM, 9)
    columns = {
        "mag_b": l0["mag_b"], "mag_gamma": l0["mag_gamma"], "mag_beta": l0["mag_beta"], "mag_mean": l0["mag_mean"],
        "mag_var": l0["mag_var"], "ph_b": l0["phase_b"][:P], "ph_gamma": l0["phase_gamma"][:P],
        "ph_beta": l0["phase_beta"][:P], "ph_mean": l0["phase_mean"][:P], "ph_var": l0["phase_var"][:P],
        "alpha": np.repeat(l0["alpha"], P), "l1_dtb0": l1["dt_b"][:2].ravel(), "l1_dtb1": l1["dt_b"][2:].ravel(),
        "l1_A0": A[:2].ravel(), "l1_A1": A[2:].ravel(), "l1_gb": np.concatenate([l1["ln_g"], l1["ln_b"]]),
        "l1_scale": twice(l1["scale_w"].ravel()), "l1_cb": twice(l1["conv_b"]), "l1_cv1b": twice(l1["cv1_b"]),
        "cv2_b": l1["cv2_b"], "cpe1_b": l2["cpe1_b"], "n1_g": l2["n1_g"], "n1_b": l2["n1_b"], "in_b": l2["inproj_b"],
        "act_b": l2["actproj_b"], "dwc_b": l2["dwc_b"], "q_b": l2["qk_b"][:P], "lepe_b": l2["lepe_b"],
        "out_b": l2["outproj_b"], "cpe2_b": l2["cpe2_b"], "n2_g": l2["n2_g"], "n2_b": l2["n2_b"], "fc2_b": l2["fc2_b"],
        "fc1_b": l2["fc1_b"].reshape(4, P).T,
        "taps": np.concatenate([l2[c + "_w"].reshape(P, 9) for c in ("cpe1", "dwc", "lepe", "cpe2")], axis=1),
        "l1taps": np.concatenate([np.concatenate([cw[:, 0:3], cw[:, 3:6]]), np.concatenate([cw[:, 6:9]] * 2)], axis=1),
        "l1_D": twice(Ds.T),
    }
    a["cols"] = np.concatenate([columns[n].reshape(P, -1) for n in HOST_COLS], axis=1)
    return {k: np.ascontiguousarray(v) for k, v in a.items()}


def kernel(**inputs):
    import concourse.bacc as bacc
    from concourse.bass_utils import run_bass_kernel_spmd

    arrays = layout(inputs)
    nc = bacc.Bacc("TRN2", target_bir_lowering=False, num_devices=1)
    aps = {k: nc.dram_tensor("in_" + k, v.shape, mybir.dt.from_np(v.dtype), kind="ExternalInput").ap()
           for k, v in arrays.items()}
    out = nc.dram_tensor("out", arrays["x"].shape, F32, kind="ExternalOutput").ap()
    build(nc, aps, out)
    got = run_bass_kernel_spmd(nc, [{"in_" + k: v for k, v in arrays.items()}], core_ids=[0])
    return got.results[0]["out"]
```

```python
from contextlib import ExitStack

import numpy as np

import concourse.bass as bass
from concourse import mybir

F32 = mybir.dt.float32
BF16 = mybir.dt.bfloat16
ACT = mybir.ActivationFunctionType
ALU = mybir.AluOpType
ds = bass.ds

P = 128
CM = 64
ROWS = 8
HALF = ROWS // 2
BANK = 512
CREDIT = 3
HEADS = 8
RANK = 8
EPS = 1e-5

TAPS = [(0, 0), (0, -1), (0, 1), (-1, 0), (1, 0), (-1, -1), (-1, 1), (1, -1), (1, 1)]
TERM_TAPS = (1, 2)
VECTOR_TAPS = (3, 4, 5, 6)
CHAIN = 1 + len(TERM_TAPS) + len(VECTOR_TAPS)


HOST_COLS = ["mag_b", "mag_gamma", "mag_beta", "mag_mean", "mag_var", "ph_b", "ph_gamma", "ph_beta", "ph_mean", "ph_var",
             "alpha", "l1_dtb0", "l1_dtb1", "l1_A0", "l1_A1", "l1_gb", "l1_scale", "l1_cb", "l1_cv1b", "cv2_b",
             "cpe1_b", "n1_g", "n1_b", "in_b", "act_b", "dwc_b", "q_b", "lepe_b", "out_b", "cpe2_b", "n2_g", "n2_b",
             "fc2_b", "fc1_b", "taps", "l1taps", "l1_D"]
CHIP_COLS = ["fc1_o", "mag_s", "mag_o", "mag_ns", "mag_no", "ph_s", "ph_o", "ph_ns", "ph_no", "nalpha", "xc_b", "z_b",
             "in_o", "act_o", "q_b1", "q_nb", "w3_s", "spare", "zero", "one", "eps", "tiny", "Dsum", "root", "root2"]


def tap_column(tap):
    return 3 * (tap[0] + 1) + tap[1] + 1


def pipelined(eng, count, stages):
    deepest = max(lag for lag, _ in stages)

    def step(t, parity, whole):
        for lag, stage in stages:
            if whole or 0 <= t - lag < count:
                stage(t - lag, (parity - lag) % 2)

    start = min(deepest + 1, count)
    pairs = (count - 1 - start) // 2
    for t in range(start):
        step(t, t % 2, False)
    if pairs >= 2:
        with eng.Fori(0, pairs, 1) as k:
            for u in range(2):
                step(2 * k + (start + u), (start + u) % 2, True)
        start += 2 * pairs
    for t in range(start, count + deepest):
        step(t, t % 2, False)


def build(nc, t, out):
    B, _, S, _ = t["x"].shape
    NB = S // ROWS
    N = S * S
    BLK = ROWS * S
    HC = HALF * S
    SP = S + 2
    NT = BLK // P
    REGION = max(SP * SP, 25 * BLK // 2)
    QUARTER = BLK // 4

    def done(i, b):
        return i * NB + (b + (1 + CREDIT))

    def steps(i, b, each, step):
        return i * (NB * each) + (b * each + step)

    def landed(i, b, p):
        return i * (8 * NB) + (b * 8 + (16 - 8 * p))

    ctx = ExitStack()
    with ctx:
        def sb(name, shape, dt=F32):
            return ctx.enter_context(nc.sbuf_tensor(name, shape, dt))

        def sem(name):
            return ctx.enter_context(nc.semaphore(name))

        psum = ctx.enter_context(nc.psum_tensor("psum", [P, 8, BANK], F32))

        def pair(bank):
            return psum[:, bank:bank + 2, 0:HC]

        def rows_of(ap):
            return ap.rearrange("p a (r w) -> p a r w", w=S)

        R = [sb(f"region{k}", [P, REGION]) for k in range(4)]

        def padded(k):
            return R[k][:, 0:SP * SP].rearrange("p (h w) -> p h w", w=SP)

        def flat(k, b):
            return R[k][:, ds(BLK * b, BLK)]

        def prow(k, b, dh=0, dw=0, rows=ROWS, skip=0):
            return padded(k)[:, ds(ROWS * b + (1 + dh + skip), rows), 1 + dw:1 + dw + S]

        work = sb("work", [P, 8 * BLK])
        relu_tiles = sb("relu_tiles", [P, 2 * BLK])

        def tile(n):
            return work[:, n * BLK:(n + 1) * BLK]

        def region_tile(k, n):
            return R[k][:, n * BLK:(n + 1) * BLK]

        def halves(ap):
            return ap.rearrange("p (a c) -> p a c", a=2)

        def by_rows(ap):
            return ap.rearrange("p (a r w) -> p a r w", a=2, w=S)

        names = {}

        def mat(name, cols=P, rows=P, dt=F32):
            names[name] = sb("m_" + name, [rows, cols], dt)
            return names[name]

        ident = mat("ident")
        cen128 = mat("cen128")
        avg128 = mat("avg128")
        headmask = mat("headmask")
        rot = mat("rot")
        rotT = mat("rotT")
        ph_a, ph_b, magT = mat("ph_a"), mat("ph_b"), mat("magT")
        w_xc, w_z = mat("w_xc"), mat("w_z")
        same_half = mat("same_half")
        dwl1 = mat("dwl1")
        w_dt = [mat(f"w_dt{n}") for n in range(2)]
        w_B = [mat(f"w_B{n}") for n in range(2)]
        w_C = [mat(f"w_C{n}") for n in range(2)]
        cen64 = mat("cen64")
        w_l1out = mat("w_l1out")
        convs = ("cpe1", "dwc", "lepe", "cpe2")
        diag = {c: [mat(f"{c}_{n}") for n in range(9 - CHAIN)] for c in convs}
        w_in, w_act, w_q, w_out = mat("w_in"), mat("w_act"), mat("w_q"), mat("w_out")
        w_k = mat("w_k")
        kbias = mat("kbias")
        kv, kv_rot, kmean = mat("kv"), mat("kv_rot"), mat("kmean")
        fc1 = mat("fc1", 4 * P)
        fc2 = mat("fc2", 4 * P)
        w3 = mat("w3", 9 * P, dt=BF16)

        def tapped(i, conv, b):
            return i * (4 * NB) + (b + (convs.index(conv) * NB + 1 + CREDIT))

        def termed(i, conv, b):
            return i * (3 * NB) + (b + (("cpe1", "dwc", "cpe2").index(conv) * NB + 1))

        groups = {"fc1_b": 4, "taps": 36, "l1taps": 6, "l1_D": 4, "fc1_o": 4}
        at, width = {}, 0
        for name in HOST_COLS + CHIP_COLS:
            at[name] = width
            width += groups[name] if name in groups else 1
        host_width = at[CHIP_COLS[0]]
        cols = sb("cols", [P, width])

        def col(name, n=0, rows=slice(0, P)):
            return cols[rows, at[name] + n:at[name] + n + 1]

        def tap_weight(conv, tap):
            return col("taps", 9 * convs.index(conv) + tap_column(tap))

        def chain_tap(eng, i, conv, n, k, tile_of):
            def stage(b, p):
                tgt = by_row(tile_of(p))
                eng.wait_ge(tap_done[n - 1], tapped(i, conv, b))
                eng.scalar_tensor_tensor(out=tgt, in0=prow(k, b, *TAPS[n]), scalar=tap_weight(conv, TAPS[n]), in1=tgt,
                                         op0=ALU.mult, op1=ALU.add).then_inc(tap_done[n], 1)
            return stage

        def chain_tile(conv, n, p):
            return region_tile(0, 2 * n + p) if conv == "cpe2" else tile((0, 4, 6)[n] + p)

        block_signals = []

        def signal(name, owner):
            s = sem(name)
            block_signals.append((s, owner))
            return s

        setup_loaded = sem("setup_loaded")
        late_loaded = sem("late_loaded")
        setup_vec = sem("setup_vec")
        setup_act = sem("setup_act")
        setup_pe = sem("setup_pe")
        ready = sem("ready")

        x_in = [sem(f"x_in{n}") for n in range(2)]
        l0_high = signal("l0_high", "v")
        l0_mm = signal("l0_mm", "p")
        l0_relu = signal("l0_relu", "a")
        l0_out = signal("l0_out", "v")
        a_mm = signal("a_mm", "p")
        a_xc = signal("a_xc", "v")
        a_act = signal("a_act", "a")
        b_first = signal("b_first", "a")
        b_second = signal("b_second", "a")
        b_taps = [signal(f"b_taps{n}", "g" if n == 1 else "v") for n in range(1, 5)]
        b_mm = signal("b_mm", "p")
        b_act = signal("b_act", "a")
        c_sets = []
        for d in "fr":
            c_sets.append({k: signal(f"c{d}_{k}", o) for k, o in (
                ("dt", "p"), ("B", "p"), ("C", "p"), ("abs", "a"), ("exp", "a"), ("relu", "a"), ("log", "a"), ("step", "v"),
                ("decay", "a"),
                ("du", "g"), ("bu", "v"), ("h", "v"), ("hc", "v"), ("y", "g")) if d + k != "fy"})
        d_rows = signal("d_rows", "v")
        d_turned = signal("d_turned", "a")
        d_yc = signal("d_yc", "p")
        d_sq = signal("d_sq", "a")
        d_var = signal("d_var", "p")
        d_log = signal("d_log", "a")
        d_rstd = signal("d_rstd", "a")
        d_norm = signal("d_norm", "v")
        d_gate = signal("d_gate", "g")
        d_mm = signal("d_mm", "p")
        d_out = signal("d_out", "v")
        e1 = {k: signal(f"e1_{k}", o) for k, o in (
            ("conv", "p"), ("t", "v"), ("yc", "p"), ("sq", "a"), ("var", "p"), ("log", "a"), ("rstd", "a"), ("tn", "v"))}
        e2_mm = signal("e2_mm", "p")
        e2_ti = signal("e2_ti", "v")
        e2_act = signal("e2_act", "a")
        e2_conv = signal("e2_conv", "p")
        e2_sum = signal("e2_sum", "v")
        e2_v = signal("e2_v", "a")
        f1_stage = signal("f1_stage", "a")
        f1_mm = signal("f1_mm", "p")
        f1_bias = signal("f1_bias", "v")
        f1_min = signal("f1_min", "v")
        f1_exp = signal("f1_exp", "a")
        f1_vT = signal("f1_vT", "a")
        f1_k = signal("f1_k", "v")
        f1_kc = signal("f1_kc", "v")
        f1_ks = signal("f1_ks", "v")
        f1_kv = signal("f1_kv", "p")
        f1_ksum = signal("f1_ksum", "g")
        f1_tab = [sem(f"f1_tab{n}") for n in range(2)]
        image_begun = sem("image_begun")
        kv_pe = sem("kv_pe")
        kv_vec = sem("kv_vec")
        f2_q = signal("f2_q", "p")
        f2_min = signal("f2_min", "a")
        f2_exp = signal("f2_exp", "a")
        f2_phi = signal("f2_phi", "v")
        f2_qc = signal("f2_qc", "g")
        f2_qs = signal("f2_qs", "g")
        f2_den = signal("f2_den", "p")
        f2_log = signal("f2_log", "a")
        f2_z = signal("f2_z", "a")
        f2_num = signal("f2_num", "p")
        f2_nz = signal("f2_nz", "v")
        f2_conv = signal("f2_conv", "p")
        f2_lepe = signal("f2_lepe", "v")
        f2_sum = signal("f2_sum", "g")
        f2_ta = signal("f2_ta", "g")
        f2_out = signal("f2_out", "p")
        f2_t2 = signal("f2_t2", "v")
        f2_tab = [sem(f"f2_tab{n}") for n in range(2)]
        g_fc1 = signal("g_fc1", "p")
        g_gelu = signal("g_gelu", "a")
        g_fc2 = signal("g_fc2", "p")
        g_x3 = signal("g_x3", "v")
        g_tap7 = signal("g_tap7", "v")
        g_t = signal("g_t", "v")
        g_yc = signal("g_yc", "p")
        g_sq = signal("g_sq", "a")
        g_var = signal("g_var", "p")
        g_log = signal("g_log", "a")
        g_rstd = signal("g_rstd", "a")
        g_tn = signal("g_tn", "v")
        g_sign = signal("g_sign", "a")
        h_mm = signal("h_mm", "p")
        h_scale = signal("h_scale", "a")
        h_store = [sem(f"h_store{n}") for n in range(2)]
        borders = sem("borders")
        term_done = {n: sem(f"term_done{n}") for n in TERM_TAPS}
        tap_done = [sem(f"tap_done{n}") for n in range(CHAIN)]
        l0_steps = sem("l0_steps")
        l0_join = sem("l0_join")
        setup_steps = sem("setup_steps")

        def credit(eng, owner):
            for s, o in block_signals:
                if o == owner:
                    eng.sem_inc(s, CREDIT * (4 if s is g_fc1 or s is g_gelu else 1))
            for n, s in enumerate(tap_done):
                if owner == ("a" if n == 0 else "g" if n in TERM_TAPS else "v"):
                    eng.sem_inc(s, CREDIT)

        def all_done(eng, i, *signals):
            eng.wait_ge(ready, 1)
            for s in signals:
                k = 4 if s is g_fc1 or s is g_gelu else 1
                eng.wait_ge(s, i * (NB * k) + (NB + CREDIT) * k)

        G_ALL = (g_fc1, g_gelu, g_fc2, g_x3, g_sign)

        rhs_l1 = R[0][0:CM, 0:4 * CM]
        cv1 = R[0][0:CM, 256:384]
        opj2 = R[0][0:CM, 384:512]
        cv2T = R[0][0:CM, 512:640]
        cv2Ts = R[0][0:CM, 640:768]
        xp_r = R[1][0:RANK, 0:4 * P]
        dt_r = R[1][0:RANK, 512:512 + 4 * P]
        bc_r = R[1][0:2, 1024:1024 + 4 * P]
        half_ones = R[1][0:2, 1536:1664]
        ones_row = R[1][0:1, 1664:1792]
        kb_row = R[1][0:1, 1792:1920]
        w3_nat = R[2][:, 0:9 * P]
        w3_T = R[2][:, 9 * P:18 * P]
        raw_in = R[3][:, 128:256]
        raw_act = R[3][:, 256:384]
        raw_fc1 = R[3][:, 384:896]
        loads = [
            (ident[:, :], t["c_ident"]), (cen128[:, :], t["c_cen128"]), (avg128[:, :], t["c_avg128"]),
            (headmask[:, :], t["c_headmask"]), (rot[:, :], t["c_rot"]), (rotT[:, :], t["c_rotT"]),
            (cen64[:, :], t["c_cen64"]), (same_half[:, :], t["c_e2"]),
            (ph_a[:, :], t["ph_aT"]), (ph_b[:, :], t["ph_bT"]), (magT[:, :], t["magT"]),
            (rhs_l1[:, 0:64], t["inprojT"][:, 0:64]), (rhs_l1[:, 64:128], t["inprojT"][:, 0:64]),
            (rhs_l1[:, 128:192], t["inprojT"][:, 64:128]), (rhs_l1[:, 192:256], t["inprojT"][:, 64:128]),
            (cv1, t["cv1_w"]), (opj2[:, 0:64], t["out_proj"]), (opj2[:, 64:128], t["out_proj"]), (cv2T, t["cv2T"]),
            (raw_in, t["inproj_w"]), (raw_act, t["actproj_w"]), (raw_fc1, t["fc1_w"]),
            (fc2[:, :].rearrange("p (j o) -> p j o", j=4), t["fc2_w"].rearrange("(j p) o -> p j o", p=P)),
            (w_q[:, :], t["qk_w"][:, 0:P]), (w_k[:, :], t["qk_w"][:, P:2 * P]),
            (w_out[:, :], t["outproj_w"]), (kb_row, t["kb_row"]), (half_ones, t["c_half"]),
            (w3_nat, t["w3_nat"]), (w3_T, t["w3_T"]),
            (cols[:, 0:host_width], t["cols"]),
        ]
        late_loads = []
        for k in range(4):
            lo, hi = P * k + CM * (k % 2), P * k + CM * (k % 2) + CM
            late_loads.append((xp_r[:, lo:hi], t["x_proj"][k, 0:RANK, :]))
            late_loads.append((dt_r[:, lo:hi], t["dt_wT"][k]))
        for sweep in range(2):
            for half in range(2):
                for what in range(2):
                    c0 = P * (2 * sweep + what) + CM * half
                    late_loads.append((bc_r[half:half + 1, c0:c0 + CM],
                                       t["x_proj"][2 * sweep + half, RANK + what:RANK + what + 1, :]))


        def scan_tap(n):
            return (-1, n - 1) if n < 3 else (1, n - 4)

        def by_row(ap):
            return ap.rearrange("p (r w) -> p r w", w=S)

        def is_first(b):
            return isinstance(b, int) and b == 0

        def following(b):
            return b if isinstance(b, int) and b == NB - 1 else b + 1

        def kcs(p):
            return R[3][:, (2 + 2 * p) * BLK:(4 + 2 * p) * BLK].rearrange("p (n c) -> p n c", n=NT)

        def tok_table(p, which):
            v = region_tile(3, 6 + p).rearrange("p (s n j) -> p s n j", s=2, n=NT)[:, which]
            return v.unsqueeze(3).broadcast_to((P, NT, CM, 2))

        def by_pairs(ap):
            return ap.rearrange("p n (j e) -> p n j e", e=2)

        def by_tile(ap):
            return ap.rearrange("p (n c) -> p n c", n=NT)

        def signs():
            return R[1][:, :].bitcast(BF16)[:, 0:SP * SP].rearrange("p (h w) -> p h w", w=SP)

        def pad_rows(k, b, parts, up=0):
            return padded(k)[parts, ds(ROWS * b + (1 - up), ROWS), 1:1 + S].rearrange("p (a r) w -> p a r w", a=2)

        def token_psum(p):
            v = psum[:, 3 * p:3 * p + 3, :].rearrange("p a c -> p (a c)")[:, 0:NT * 2 * P]
            return v.rearrange("p (n c) -> p n c", c=2 * P)

        def quarter(n):
            return R[2][:, n * QUARTER:(n + 1) * QUARTER]

        x_tile = [region_tile(2, p) for p in range(2)]
        pair_sum = [R[2][:, (8 + 2 * p) * QUARTER:(10 + 2 * p) * QUARTER] for p in range(2)]
        quad_sum = [quarter(12 + p) for p in range(2)]
        low_pos = [quarter(14 + p) for p in range(2)]
        low_wide = [R[2][:, (16 + 2 * p) * QUARTER:(18 + 2 * p) * QUARTER] for p in range(2)]
        high = [R[2][:, 5 * BLK + p * 9 * S:5 * BLK + (p + 1) * 9 * S].rearrange("p (r w) -> p r w", w=S)
                for p in range(2)]
        hs_pos = [R[2][:, (30 + 4 * p) * QUARTER:(34 + 4 * p) * QUARTER] for p in range(2)]
        hs_neg = [R[2][:, (38 + 4 * p) * QUARTER:(42 + 4 * p) * QUARTER] for p in range(2)]
        low_neg = [quarter(46 + p) for p in range(2)]
        out_low = R[2][:, 48 * QUARTER:50 * QUARTER]

        def sweep_block(sweep, b):
            return b if sweep == 0 else b * (-1) + (NB - 1)

        block = ctx.enter_context(nc.Block())

        @block.sync
        def _(sp):
            for dst, src in loads:
                sp.dma_start(dst, src).then_inc(setup_loaded, 16)
            sp.wait_ge(setup_vec, 1)
            for dst, src in late_loads:
                sp.dma_start(dst, src).then_inc(late_loaded, 16)
            for p in range(2):
                sp.sem_inc(h_store[p], 16)
            sp.wait_ge(ready, 1)
            with sp.Fori(0, B, 1) as i:
                def load_x(b, p):
                    sp.wait_ge(l0_high, done(i, b - 2))
                    sp.dma_start(x_tile[p], t["x"][ds(i, 1), :, ds(ROWS * b, ROWS), :]
                                 .rearrange("a c h w -> (a c) (h w)")).then_inc(x_in[p], 16)

                def load_tok_table(b, p):
                    sp.wait_ge(f1_kc, done(i, b - 2))
                    sp.wait_ge(f1_ks, done(i, b - 2))
                    sp.dma_start(region_tile(3, 6 + p), t["tab_tok"][ds(b, 1), :, :].rearrange("a p n -> (a p) n"))\
                        .then_inc(f1_tab[p], 16)

                def load_ch_table(b, p):
                    sp.wait_ge(f2_qc, done(i, b - 2))
                    sp.wait_ge(f2_qs, done(i, b - 2))
                    sp.dma_start(R[3][:, 2 * p * BLK:(2 * p + 2) * BLK],
                                 t["tab_ch"][ds(b, 1), :, :].rearrange("a p n -> (a p) n")).then_inc(f2_tab[p], 16)

                def store(b, p):
                    sp.wait_ge(h_scale, done(i, b))
                    sp.dma_start(out[ds(i, 1), :, ds(ROWS * b, ROWS), :].rearrange("a c h w -> (a c) (h w)"),
                                 tile(p)).then_inc(h_store[p], 16)

                all_done(sp, i - 1, *G_ALL)
                pipelined(sp, NB, [(0, load_x)])
                sp.wait_ge(e2_v, done(i, NB - 3))
                pipelined(sp, NB, [(0, load_tok_table)])
                all_done(sp, i, f1_kv)
                pipelined(sp, NB, [(0, load_ch_table)])
                pipelined(sp, NB, [(0, store)])
            for p in range(2):
                sp.wait_ge(h_store[p], 16 + B * NB // 2 * 16)

        @block.gpsimd
        def _(g):
            credit(g, "g")
            g.wait_ge(ready, 1)
            with g.Fori(0, B, 1) as i:
                def clear_frame(image, last=1):
                    g.memset(image[:, 0:1, :], 0.0)
                    g.memset(image[:, SP - last:SP, :], 0.0)
                    g.memset(image[:, 1:SP - last, 0:1], 0.0)
                    g.memset(image[:, 1:SP - last, SP - 1:SP], 0.0).then_inc(borders, 1)

                all_done(g, i - 1, *G_ALL)
                g.sem_inc(image_begun, 1)
                clear_frame(padded(3), last=2)

                def first_sum(b, p):
                    g.wait_ge(b_first, done(i, b))
                    g.wait_ge(b_second, done(i, b))
                    g.wait_ge(b_taps[3], done(i, b - 2))
                    g.tensor_tensor(tile(4 + p), tile(p), tile(2 + p), ALU.add).then_inc(b_taps[0], 1)

                pipelined(g, NB, [(1, first_sum)])

                for sweep in range(2):
                    c = c_sets[sweep]

                    def du(b, p):
                        g.wait_ge(c["step"], done(i, b))
                        g.wait_ge(c["h"], done(i, b - 2))
                        g.tensor_tensor(tile(2 + p), tile(p), flat(2, sweep_block(sweep, b)), ALU.mult)\
                            .then_inc(c["du"], 1)

                    def add_y(b, p):
                        y = flat(3, sweep_block(sweep, b))
                        g.wait_ge(c["hc"], done(i, b))
                        g.tensor_tensor(y, y, tile(4 + p), ALU.add).then_inc(c["y"], 1)

                    if sweep == 0:
                        pipelined(g, NB, [(0, du)])
                    else:
                        pipelined(g, NB, [(2, add_y), (0, du)])

                def gate(b, p):
                    z = flat(1, b)[0:CM]
                    g.wait_ge(d_norm, done(i, b))
                    g.tensor_tensor(z, tile(2 + p)[0:CM], z, ALU.mult).then_inc(d_gate, 1)

                pipelined(g, NB, [(0, gate)])

                def add_term(conv, n):
                    def stage(b, p):
                        g.wait_ge(term_done[n], termed(i, conv, b))
                        g.wait_ge(tap_done[n - 1], tapped(i, conv, b))
                        g.tensor_tensor(chain_tile(conv, n, p), chain_tile(conv, n - 1, p), chain_tile(conv, n, p),
                                        ALU.add).then_inc(tap_done[n], 1)
                    return stage

                taps = [add_term("cpe1", tap) for tap in TERM_TAPS]
                pipelined(g, NB, [(0, tap) for tap in taps])

                all_done(g, i, d_mm)
                clear_frame(padded(3))
                clear_frame(padded(1))

                taps = [add_term("dwc", tap) for tap in TERM_TAPS]
                pipelined(g, NB, [(3, tap) for tap in taps])

                def ksum(b, p):
                    g.wait_ge(ready, 1)
                    g.wait_ge(f1_k, done(i, b))
                    if isinstance(b, int) and b == 0:
                        g.tensor_copy(tile(6), tile(p)).then_inc(f1_ksum, 1)
                    else:
                        g.wait_ge(f1_ksum, done(i, b - 1))
                        g.tensor_tensor(tile(6), tile(6), tile(p), ALU.add).then_inc(f1_ksum, 1)

                pipelined(g, NB, [(3, ksum)])

                def turned(b, p):
                    g.wait_ge(f2_phi, done(i, b))
                    g.wait_ge(f2_tab[p], landed(i, b, p))
                    g.wait_ge(f2_num, done(i, b - 2))
                    g.tensor_tensor(region_tile(3, 4 + p), tile(p), region_tile(3, 2 * p), ALU.mult).then_inc(f2_qc, 1)
                    g.tensor_tensor(region_tile(3, 6 + p), tile(p), region_tile(3, 2 * p + 1), ALU.mult).then_inc(f2_qs, 1)

                def ta(b, p):
                    g.wait_ge(f2_nz, done(i, b))
                    g.wait_ge(f2_lepe, done(i, b))
                    g.tensor_tensor(tile(2 + p), tile(6 + p), tile(2 + p), ALU.add).then_inc(f2_sum, 1)
                    g.wait_ge(f2_sum, done(i, b))
                    g.tensor_tensor(tile(2 + p), tile(2 + p), flat(2, b), ALU.mult).then_inc(f2_ta, 1)

                pipelined(g, NB, [(3, ta), (1, turned)])

                taps = [add_term("cpe2", tap) for tap in TERM_TAPS]
                pipelined(g, NB, [(0, tap) for tap in taps])

                all_done(g, i, g_t)
                clear_frame(signs())
                clear_frame(padded(0))

        @block.scalar
        def _(a):
            credit(a, "a")
            a.wait_ge(setup_loaded, 16 * len(loads))
            a.wait_ge(setup_vec, 2)
            a.activation(col("root"), col("mag_var"), ACT.Sqrt, bias=col("eps"))
            a.activation(col("root2"), col("ph_var"), ACT.Sqrt, bias=col("eps"))
            a.activation(w3[:, :], w3_T, ACT.Sign)
            a.activation(w3_nat, w3_nat, ACT.Abs, accum_out=col("w3_s"))
            a.activation(col("l1_A0"), col("l1_A0"), ACT.Exp)
            a.activation(col("l1_A1"), col("l1_A1"), ACT.Exp).then_inc(setup_act, 1)
            a.wait_ge(ready, 1)
            with a.Fori(0, B, 1) as i:
                def relus(b, p):
                    a.wait_ge(l0_mm, done(i, b))
                    a.wait_ge(l0_out, done(i, b - 2))
                    low = psum[:, 2, 0:QUARTER]
                    a.activation(low_pos[p], low, ACT.Relu, bias=col("mag_o"), scale=col("mag_s"))
                    a.activation(low_neg[p], low, ACT.Relu, bias=col("mag_no"), scale=col("mag_ns"))
                    a.activation(halves(hs_pos[p]), pair(0), ACT.Relu, bias=col("ph_o"), scale=col("ph_s"))
                    a.activation(halves(hs_neg[p]), pair(0), ACT.Relu, bias=col("ph_no"), scale=col("ph_ns"))\
                        .then_inc(l0_relu, 1)

                def silu_z(b, p):
                    a.wait_ge(a_mm, done(i, b))
                    a.activation(pad_rows(3, b, slice(CM, P), up=1), rows_of(pair(3))[CM:P], ACT.Identity,
                                 bias=col("xc_b", rows=slice(CM, P)))
                    a.activation(halves(flat(1, b)), pair(5), ACT.Silu, bias=col("z_b")).then_inc(a_act, 1)

                a.wait_ge(borders, i * 5 + 1)
                pipelined(a, NB, [(3, silu_z), (0, relus)])

                def silu_u(b, p):
                    a.wait_ge(b_mm, done(i, b))
                    a.activation(halves(flat(2, b)[0:CM]), pair(2 * p)[0:CM], ACT.Silu, bias=col("l1_cb", rows=slice(0, CM)))
                    turned = R[2][CM:P, 0:N].rearrange("p (w h) -> p h w", h=S)[:, ds(ROWS * b, ROWS), :]
                    a.activation(turned.rearrange("p (a r) w -> p a r w", a=2), rows_of(pair(2 * p))[CM:P], ACT.Silu,
                                 bias=col("l1_cb", rows=slice(CM, P))).then_inc(b_act, 1)

                def first_terms(b, p):
                    a.wait_ge(a_xc, done(i, following(b)))
                    a.wait_ge(b_taps[0], done(i, b - 2))
                    for n, signal_of in enumerate((b_first, b_second)):
                        a.activation(by_row(tile(2 * n + p)), prow(3, b, *scan_tap(n)), ACT.Copy, scale=col("l1taps", n))\
                            .then_inc(signal_of, 1)

                for p in range(2):
                    a.wait_ge(h_store[p], i * (8 * NB) + 16)
                pipelined(a, NB, [(0, first_terms), (3, silu_u)])

                for sweep in range(2):
                    c = c_sets[sweep]

                    def soft(b, p):
                        a.wait_ge(c["dt"], done(i, b))
                        a.wait_ge(c["decay"], done(i, b - 2))
                        a.wait_ge(c["du"], done(i, b - 2))
                        if sweep == 1 and is_first(b):
                            a.wait_ge(c_sets[0]["du"], done(i, NB - 1))
                        a.activation(halves(tile(p)), pair(2 * p), ACT.Abs, bias=col(f"l1_dtb{sweep}")).then_inc(c["abs"], 1)
                        a.wait_ge(c["abs"], done(i, b))
                        a.activation(tile(p), tile(p), ACT.Exp, scale=-1.0).then_inc(c["exp"], 1)
                        a.wait_ge(c["step"], done(i, b - 2))
                        a.activation(halves(relu_tiles[:, BLK * p:BLK * (p + 1)]), pair(2 * p), ACT.Relu,
                                     bias=col(f"l1_dtb{sweep}")).then_inc(c["relu"], 1)
                        a.wait_ge(c["exp"], done(i, b))
                        a.activation(tile(p), tile(p), ACT.Ln, bias=col("one")).then_inc(c["log"], 1)

                    def decay(b, p):
                        a.wait_ge(c["step"], done(i, b))
                        a.wait_ge(c["hc" if sweep == 0 else "y"], done(i, b - 2))
                        a.activation(tile(4 + p), tile(p), ACT.Exp, scale=col(f"l1_A{sweep}")).then_inc(c["decay"], 1)

                    a.preload_act_table_set("natural_log_exp_and_others")
                    pipelined(a, NB, [(2, decay), (0, soft)])

                def turned(b, p):
                    a.wait_ge(d_yc, done(i, b - 2))
                    y = R[3][CM:P, 0:N].rearrange("p (w h) -> p h w", h=S)[:, ds(ROWS * b, ROWS), :]
                    a.activation(by_row(tile(4 + p))[CM:P], y, ACT.Copy).then_inc(d_turned, 1)

                def squares(b, p):
                    a.wait_ge(d_yc, done(i, b))
                    a.wait_ge(d_norm, done(i, b - 2))
                    a.activation(halves(tile(p)), pair(2 * p), ACT.Square).then_inc(d_sq, 1)

                def root(b, p):
                    a.wait_ge(d_var, done(i, b))
                    a.activation(halves(tile(p)), pair(4), ACT.Ln, bias=col("eps")).then_inc(d_log, 1)
                    a.wait_ge(d_log, done(i, b))
                    a.activation(tile(p), tile(p), ACT.Exp, scale=-0.5).then_inc(d_rstd, 1)

                a.preload_act_table_set("natural_log_exp_and_others")
                all_done(a, i, c_sets[1]["y"])
                pipelined(a, NB, [(0, turned), (2, root), (1, squares)])

                def first_tap(conv, k, tile_of, free):
                    def stage(b, p):
                        free(b)
                        a.activation(by_row(tile_of(p)), prow(k, b), ACT.Identity, scale=tap_weight(conv, TAPS[0]),
                                     bias=col(conv + "_b")).then_inc(tap_done[0], 1)
                    return stage

                def terms(conv, k, lag, rows, used):
                    def free(b):
                        a.wait_ge(tap_done[1], tapped(i, conv, b - 2))
                        a.wait_ge(rows, done(i, following(b)))

                    return [(lag, first_tap(conv, k, lambda p: chain_tile(conv, 0, p), free))] +\
                        [(lag, term(conv, n, k, used)) for n in TERM_TAPS]

                def term(conv, n, k, used):
                    def stage(b, p):
                        if n == TERM_TAPS[-1]:
                            a.wait_ge(used, done(i, b - 2))
                        else:
                            a.wait_ge(tap_done[n + 1], tapped(i, conv, b - 2))
                        a.activation(by_row(chain_tile(conv, n, p)), prow(k, b, *TAPS[n]), ACT.Copy,
                                     scale=tap_weight(conv, TAPS[n])).then_inc(term_done[n], 1)
                    return stage

                def squares(b, p):
                    a.wait_ge(e1["yc"], done(i, b))
                    a.wait_ge(e1["tn"], done(i, b - 2))
                    a.activation(halves(tile(2 + p)), pair(2 + 2 * p), ACT.Square).then_inc(e1["sq"], 1)

                def root(b, p):
                    a.wait_ge(e1["var"], done(i, b))
                    a.activation(halves(tile(2 + p)), pair(6), ACT.Ln, bias=col("eps")).then_inc(e1["log"], 1)
                    a.wait_ge(e1["log"], done(i, b))
                    a.activation(tile(2 + p), tile(2 + p), ACT.Exp, scale=-0.5).then_inc(e1["rstd"], 1)

                all_done(a, i, d_gate)
                a.preload_act_table_set("natural_log_exp_and_others")
                pipelined(a, NB, terms("cpe1", 0, 0, d_out, e1["t"]) + [(3, squares), (4, root)])

                def silu_act(b, p):
                    a.wait_ge(e2_mm, done(i, b))
                    a.activation(halves(flat(2, b)), pair(2), ACT.Silu, bias=col("act_o")).then_inc(e2_act, 1)

                def silu_v(b, p):
                    a.wait_ge(e2_sum, done(i, b))
                    a.activation(prow(0, b), by_row(tile(2 + p)), ACT.Silu).then_inc(e2_v, 1)

                a.wait_ge(borders, i * 5 + 3)
                pipelined(a, NB, terms("dwc", 3, 3, e2_ti, e2_sum) + [(5, silu_v), (0, silu_act)])

                def stage(b, p):
                    a.wait_ge(e2_v, done(i, b))
                    a.wait_ge(f1_mm, done(i, b - 2))
                    a.activation(by_row(region_tile(3, p)), prow(0, b), ACT.Copy).then_inc(f1_stage, 1)

                def key_exp(b, p):
                    kin = token_psum(p)
                    a.wait_ge(f1_min, done(i, b))
                    a.activation(tile(2 + p), tile(2 + p), ACT.Exp).then_inc(f1_exp, 1)
                    a.wait_ge(f1_mm, done(i, b))
                    a.wait_ge(f1_kv, done(i, b - 2))
                    a.activation(by_tile(tile(4 + p)), kin[:, :, P:2 * P], ACT.Copy).then_inc(f1_vT, 1)

                a.preload_act_table_set("natural_log_exp_and_others")
                pipelined(a, NB, [(0, stage), (2, key_exp)])

                def query_exp(b, p):
                    a.wait_ge(f2_q, done(i, b))
                    a.wait_ge(f2_phi, done(i, b - 2))
                    a.activation(halves(region_tile(3, 8 + p)), pair(0), ACT.Relu, scale=-1.0, bias=col("q_nb"))\
                        .then_inc(f2_min, 1)
                    a.wait_ge(f2_min, done(i, b))
                    a.activation(region_tile(3, 8 + p), region_tile(3, 8 + p), ACT.Exp, scale=-1.0).then_inc(f2_exp, 1)

                def reciprocal(b, p):
                    a.wait_ge(f2_den, done(i, b))
                    a.activation(halves(region_tile(3, 10 + p)), pair(2), ACT.Ln, bias=col("tiny")).then_inc(f2_log, 1)
                    a.wait_ge(f2_log, done(i, b))
                    a.activation(region_tile(3, 10 + p), region_tile(3, 10 + p), ACT.Exp, scale=-1.0).then_inc(f2_z, 1)

                all_done(a, i, f1_kv)
                a.preload_act_table_set("natural_log_exp_and_others")
                tap = first_tap("lepe", 0, lambda p: tile(4 + p), lambda b: a.wait_ge(f2_lepe, done(i, b - 2)))
                pipelined(a, NB, [(0, tap), (2, reciprocal), (0, query_exp)])

                def g_squares(b, p):
                    a.wait_ge(g_yc, done(i, b))
                    a.wait_ge(g_tn, done(i, b - 2))
                    a.activation(halves(tile(2 + p)), pair(2), ACT.Square).then_inc(g_sq, 1)

                def g_root(b, p):
                    a.preload_act_table_set("natural_log_exp_and_others")
                    a.wait_ge(g_var, done(i, b))
                    a.activation(halves(tile(2 + p)), pair(6), ACT.Ln, bias=col("eps")).then_inc(g_log, 1)
                    a.wait_ge(g_log, done(i, b))
                    a.activation(tile(2 + p), tile(2 + p), ACT.Exp, scale=-0.5).then_inc(g_rstd, 1)

                def gelu(j):
                    def stage(b, p):
                        a.wait_ge(g_fc1, steps(i, b, 4, 4 * CREDIT + j + 1))
                        a.activation(halves(tile(4 + j)), pair(0), ACT.Gelu, bias=col("fc1_o", j)).then_inc(g_gelu, 1)
                    return stage

                def sign(b, p):
                    a.wait_ge(g_x3, done(i, b))
                    a.activation(signs()[:, ds(ROWS * b + 1, ROWS), 1:1 + S],
                                 flat(3, b).rearrange("p (r w) -> p r w", w=S), ACT.Sign).then_inc(g_sign, 1)

                all_done(a, i, f2_lepe, f2_sum)
                tap, first, second = terms("cpe2", 1, 0, f2_t2, g_t)
                pipelined(a, NB, [(4, gelu(0)), tap, (6, sign), (4, gelu(1)), first, second, (4, gelu(2)), (3, g_root),
                                  (4, gelu(3)), (2, g_squares)])

                def scale_out(b, p):
                    a.wait_ge(h_mm, done(i, b))
                    a.wait_ge(h_store[p], landed(i, b, p))
                    a.activation(halves(tile(p)), pair(2 * p), ACT.Copy, scale=col("w3_s")).then_inc(h_scale, 1)

                pipelined(a, NB, [(0, scale_out)])

        @block.tensor
        def _(pe):
            credit(pe, "p")
            pe.wait_ge(setup_vec, 3)
            pe.wait_ge(setup_loaded, 16 * len(loads))
            pe.wait_ge(late_loaded, 16 * len(late_loads))
            pe.matmul(psum[:, 0, 0:256], cv1, rhs_l1, start=True, stop=True)
            pe.matmul(psum[:, 0, 256:384], opj2, cv2Ts, start=True, stop=True)
            pe.matmul(psum[:, 0, 384:512], ones_row, kb_row, start=True, stop=True)
            for k in range(4):
                pe.matmul(psum[:, 1, P * (k // 2):P * (k // 2) + P], xp_r[:, P * k:P * (k + 1)], dt_r[:, P * k:P * (k + 1)],
                          start=(k % 2 == 0), stop=(k % 2 == 1))
            for k in range(4):
                pe.matmul(psum[:, 2, P * k:P * (k + 1)], bc_r[:, P * k:P * (k + 1)], half_ones, start=True, stop=True)
            pe.matmul(psum[:, 3, 0:1], rhs_l1[:, 0:P], col("l1_cv1b", rows=slice(0, CM)), start=True, stop=True)
            pe.matmul(psum[:, 3, 1:2], rhs_l1[:, P:2 * P], col("l1_cv1b", rows=slice(0, CM)), start=True, stop=True)
            pe.matmul(psum[:, 3, 2:3], raw_in, col("n1_b"), start=True, stop=True)
            pe.matmul(psum[:, 3, 3:4], raw_act, col("n1_b"), start=True, stop=True)
            for j in range(4):
                last = pe.matmul(psum[:, 3, 4 + j:5 + j], raw_fc1[:, P * j:P * (j + 1)], col("n2_b"), start=True, stop=True)
            last.then_inc(setup_pe, 1)
            pe.wait_ge(ready, 1)

            def product(bank, terms):
                for s in range(2):
                    for n, (weights, moving) in enumerate(terms):
                        last = pe.matmul(psum[:, bank + s, 0:HC], weights[:, :], moving(s),
                                         start=(n == 0), stop=(n == len(terms) - 1))
                return last

            def flat_rows(k, b):
                return lambda s: R[k][:, ds(BLK * b + HC * s, HC)]

            def image_rows(k, b, dh=0, dw=0):
                return lambda s: prow(k, b, dh, dw, rows=HALF, skip=HALF * s)

            def static(ap):
                return lambda s: ap[:, HC * s:HC * (s + 1)]

            def taps(conv, k, b):
                return [(d, image_rows(k, b, *tap)) for d, tap in zip(diag[conv], TAPS[CHAIN:])]

            with pe.Fori(0, B, 1) as i:
                def l0(b, p):
                    pe.wait_ge(l0_high, done(i, b))
                    pe.wait_ge(l0_relu, done(i, b - 1))
                    product(0, [(ph_a, lambda s: high[p][:, 1 + HALF * s:1 + HALF * (s + 1), :]),
                                    (ph_b, lambda s: high[p][:, HALF * s:HALF * (s + 1), :])])
                    pe.matmul(psum[:, 2, 0:QUARTER], magT[:, :], low_wide[p][:, 0::2], start=True, stop=True)\
                        .then_inc(l0_mm, 1)

                def xz(b, p):
                    pe.wait_ge(l0_out, done(i, b))
                    pe.wait_ge(a_xc, done(i, b - 1))
                    pe.wait_ge(a_act, done(i, b - 1))
                    product(3, [(w_xc, image_rows(0, b))])
                    product(5, [(w_z, image_rows(0, b))]).then_inc(a_mm, 1)

                pipelined(pe, NB, [(3, xz), (0, l0)])

                def l1_conv(b, p):
                    pe.wait_ge(b_act, done(i, b - 2))
                    pe.wait_ge(b_taps[3], done(i, b))
                    product(2 * p, [(dwl1, image_rows(3, b, *scan_tap(5))), (same_half, static(tile(6 + p)))])\
                        .then_inc(b_mm, 1)

                pipelined(pe, NB, [(3, l1_conv)])

                for sweep in range(2):
                    c = c_sets[sweep]

                    def dt(b, p):
                        pe.wait_ge(c["relu"], done(i, b - 2))
                        product(2 * p, [(w_dt[sweep], flat_rows(2, sweep_block(sweep, b)))]).then_inc(c["dt"], 1)

                    def bc(b, p):
                        if sweep == 1 and is_first(b):
                            pe.wait_ge(c_sets[0]["bu"], done(i, NB - 1))
                            pe.wait_ge(c_sets[0]["hc"], done(i, NB - 1))
                        pe.wait_ge(c["bu"], done(i, b - 1))
                        product(4, [(w_B[sweep], flat_rows(2, sweep_block(sweep, b)))]).then_inc(c["B"], 1)
                        pe.wait_ge(c["hc"], done(i, b - 1))
                        product(6, [(w_C[sweep], flat_rows(2, sweep_block(sweep, b)))]).then_inc(c["C"], 1)

                    all_done(pe, i, b_act if sweep == 0 else c_sets[0]["relu"])
                    pipelined(pe, NB, [(0, dt), (3, bc)])

                def yc(b, p):
                    pe.wait_ge(d_norm, done(i, b - 2))
                    pe.wait_ge(d_rows, done(i, b))
                    pe.wait_ge(d_turned, done(i, b))
                    product(2 * p, [(cen64, static(tile(4 + p)))]).then_inc(d_yc, 1)

                def var(b, p):
                    pe.wait_ge(d_sq, done(i, b))
                    pe.wait_ge(d_log, done(i, b - 1))
                    product(4, [(avg128, static(tile(p)))]).then_inc(d_var, 1)

                def l1_out(b, p):
                    pe.wait_ge(d_gate, done(i, b))
                    pe.wait_ge(d_out, done(i, b - 1))
                    product(6, [(w_l1out, flat_rows(1, b))]).then_inc(d_mm, 1)

                pipelined(pe, NB, [(4, l1_out), (2, var), (1, yc)])

                def convolve(b, p):
                    pe.wait_ge(e1["t"], done(i, b - 1))
                    pe.wait_ge(d_out, done(i, following(b)))
                    product(0, taps("cpe1", 0, b)).then_inc(e1["conv"], 1)

                def centre(b, p):
                    pe.wait_ge(e1["t"], done(i, b))
                    pe.wait_ge(e1["tn"], done(i, b - 2))
                    product(2 + 2 * p, [(cen128, image_rows(1, b))]).then_inc(e1["yc"], 1)

                def var(b, p):
                    pe.wait_ge(e1["sq"], done(i, b))
                    pe.wait_ge(e1["log"], done(i, b - 1))
                    product(6, [(avg128, static(tile(2 + p)))]).then_inc(e1["var"], 1)

                all_done(pe, i, d_norm)
                pipelined(pe, NB, [(3, centre), (4, var), (1, convolve)])

                def in_act(b, p):
                    pe.wait_ge(e2_ti, done(i, b - 1))
                    pe.wait_ge(e2_act, done(i, b - 1))
                    product(0, [(w_in, flat_rows(2, b))])
                    product(2, [(w_act, flat_rows(2, b))]).then_inc(e2_mm, 1)

                def dwc(b, p):
                    pe.wait_ge(e2_ti, done(i, following(b)))
                    pe.wait_ge(e2_sum, done(i, b - 2))
                    product(4 + 2 * p, taps("dwc", 3, b)).then_inc(e2_conv, 1)

                all_done(pe, i, e1["tn"])
                pipelined(pe, NB, [(4, dwc), (0, in_act)])

                def keys(b, p):
                    kin = token_psum(p)
                    pe.wait_ge(f1_stage, done(i, b))
                    pe.wait_ge(f1_bias, done(i, b - 2))
                    pe.wait_ge(f1_vT, done(i, b - 2))
                    for n in range(NT):
                        tokens = region_tile(3, p)[:, P * n:P * (n + 1)]
                        pe.matmul(kin[:, n, 0:P], tokens, w_k[:, :], start=True, stop=True)
                        last = pe.transpose(kin[:, n, P:2 * P], tokens, ident[:, :])
                    last.then_inc(f1_mm, 1)

                def kv_sum(b, p):
                    pe.wait_ge(f1_vT, done(i, b))
                    pe.wait_ge(f1_kc, done(i, b))
                    pe.wait_ge(f1_ks, done(i, b))
                    for n in range(NT):
                        first = isinstance(b, int) and b == 0 and n == 0
                        final = isinstance(b, int) and b == NB - 1 and n == NT - 1
                        last = pe.matmul(psum[:, 6, 0:2 * P], tile(4 + p)[:, P * n:P * (n + 1)], kcs(p)[:, n, :],
                                         start=first, stop=final)
                    last.then_inc(f1_kv, 1)

                all_done(pe, i, e2_act, e2_sum)
                pipelined(pe, NB, [(4, kv_sum), (1, keys)])

                acc = region_tile(3, 8)
                turned = region_tile(3, 9)
                pe.wait_ge(kv_vec, i * 4 + 1)
                pe.wait_ge(f1_ksum, done(i, NB - 1))
                pe.matmul(psum[:, 7, 0:P], acc[:, 0:P], ident[:, :], start=True, stop=True)
                pe.matmul(psum[:, 7, P:2 * P], acc[:, P:2 * P], ident[:, :], start=True, stop=True)
                for n in range(NT):
                    last = pe.matmul(psum[:, 6, 300:301], tile(6)[:, P * n:P * (n + 1)], col("one"),
                                     start=(n == 0), stop=(n == NT - 1))
                last.then_inc(kv_pe, 1)
                pe.wait_ge(kv_vec, i * 4 + 2)
                pe.matmul(psum[:, 0, 0:P], ident[:, :], turned[:, 0:P], start=True, stop=False)
                pe.matmul(psum[:, 0, 0:P], rotT[:, :], turned[:, P:2 * P], start=False, stop=True).then_inc(kv_pe, 1)
                pe.wait_ge(kv_vec, i * 4 + 3)
                pe.matmul(psum[:, 1, 0:P], rot[:, :], kv[:, :], start=True, stop=True).then_inc(kv_pe, 1)
                pe.wait_ge(kv_vec, i * 4 + 4)

                def query(b, p):
                    pe.wait_ge(f2_phi, done(i, b - 1))
                    product(0, [(w_q, image_rows(0, b))]).then_inc(f2_q, 1)

                def convolve(b, p):
                    pe.wait_ge(f2_lepe, done(i, b - 1))
                    product(6, taps("lepe", 0, b)).then_inc(f2_conv, 1)

                def attend(b, p):
                    pe.wait_ge(f2_phi, done(i, b))
                    pe.wait_ge(f2_t2, done(i, b - 3))
                    pe.wait_ge(f2_log, done(i, b - 1))
                    product(2, [(kmean, static(tile(p)))]).then_inc(f2_den, 1)
                    pe.wait_ge(f2_qc, done(i, b))
                    pe.wait_ge(f2_qs, done(i, b))
                    pe.wait_ge(f2_nz, done(i, b - 1))
                    product(4, [(kv, static(region_tile(3, 4 + p))), (kv_rot, static(region_tile(3, 6 + p)))])\
                        .then_inc(f2_num, 1)

                def project(b, p):
                    pe.wait_ge(f2_ta, done(i, b))
                    pe.wait_ge(f2_log, done(i, following(following(b))))
                    pe.wait_ge(f2_t2, done(i, b - 1))
                    product(2, [(w_out, static(tile(2 + p)))]).then_inc(f2_out, 1)

                pipelined(pe, NB, [(2, attend), (4, project), (0, query), (1, convolve)])

                def g_centre(b, p):
                    pe.wait_ge(g_t, done(i, b))
                    pe.wait_ge(g_tn, done(i, b - 1))
                    product(2, [(cen128, flat_rows(3, b))]).then_inc(g_yc, 1)

                def g_variance(b, p):
                    pe.wait_ge(g_sq, done(i, b))
                    pe.wait_ge(g_log, done(i, b - 1))
                    product(6, [(avg128, static(tile(2 + p)))]).then_inc(g_var, 1)

                def up(j):
                    def stage(b, p):
                        if j == 0:
                            pe.wait_ge(g_tn, done(i, b))
                        pe.wait_ge(g_gelu, steps(i, b, 4, 4 * CREDIT + j))
                        product(0, [(fc1[:, P * j:P * (j + 1)], flat_rows(2, b))]).then_inc(g_fc1, 1)
                    return stage

                def down(j):
                    def stage(b, p):
                        if j == 0:
                            pe.wait_ge(g_x3, done(i, b - 1))
                        pe.wait_ge(g_gelu, steps(i, b, 4, 4 * CREDIT + j + 1))
                        for s in range(2):
                            last = pe.matmul(psum[:, 4 + s, 0:HC], fc2[:, P * j:P * (j + 1)], static(tile(4 + j))(s),
                                             start=(j == 0), stop=(j == 3))
                        if j == 3:
                            last.then_inc(g_fc2, 1)
                    return stage

                pipelined(pe, NB, [(4, up(0)), (5, down(3)), (4, up(1)), (4, down(0)), (4, up(2)), (4, down(1)),
                                   (3, g_variance), (4, up(3)), (4, down(2)), (2, g_centre)])

                def l3(b, p):
                    pe.wait_ge(g_sign, done(i, following(b)))
                    pe.wait_ge(h_scale, done(i, b - 2))
                    for s in range(2):
                        for n, (dh, dw) in enumerate(TAPS):
                            k = tap_column((dh, dw))
                            last = pe.matmul(psum[:, 2 * p + s, 0:HC], w3[:, P * k:P * (k + 1)],
                                             signs()[:, ds(ROWS * b + (1 + dh + HALF * s), HALF), 1 + dw:1 + dw + S],
                                             start=(n == 0), stop=(n == 8))
                    last.then_inc(h_mm, 1)

                pe.wait_ge(borders, i * 5 + 4)
                pipelined(pe, NB, [(0, l3)])

        @block.vector
        def _(v):
            credit(v, "v")
            count = [0]

            def link(ins):
                count[0] += 1
                ins.then_inc(setup_steps, 1)
                v.wait_ge(setup_steps, count[0])

            v.memset(xp_r, 0.0)
            v.memset(dt_r, 0.0)
            link(v.memset(bc_r, 0.0))
            v.memset(ones_row, 1.0).then_inc(setup_vec, 1)
            v.wait_ge(setup_loaded, 16 * len(loads))
            v.memset(col("zero"), 0.0)
            v.memset(col("one"), 1.0)
            v.memset(col("tiny"), 1e-6)
            link(v.memset(col("eps"), EPS))
            v.memset(col("spare"), 0.0).then_inc(setup_vec, 1)
            link(v.tensor_scalar(cv2Ts, cv2T, col("l1_scale", rows=slice(0, CM)), None, ALU.mult))
            v.memset(col("spare"), 0.0).then_inc(setup_vec, 1)
            v.wait_ge(setup_act, 1)
            for name, root_name in (("mag", "root"), ("ph", "root2")):
                link(v.reciprocal(col(root_name), col(root_name)))
                link(v.tensor_tensor(col(name + "_s"), col(name + "_gamma"), col(root_name), ALU.mult))
                link(v.tensor_tensor(col(name + "_o"), col(name + "_b"), col(name + "_mean"), ALU.subtract))
                link(v.tensor_tensor(col(name + "_o"), col(name + "_o"), col(name + "_s"), ALU.mult))
                link(v.tensor_tensor(col(name + "_o"), col(name + "_o"), col(name + "_beta"), ALU.add))
                link(v.tensor_scalar(col(name + "_ns"), col(name + "_s"), -1.0, None, ALU.mult))
                link(v.tensor_scalar(col(name + "_no"), col(name + "_o"), -1.0, None, ALU.mult))
            v.tensor_scalar(col("nalpha"), col("alpha"), -1.0, None, ALU.mult)
            for n in range(2):
                v.tensor_scalar(col(f"l1_A{n}"), col(f"l1_A{n}"), -1.0, None, ALU.mult)
            v.tensor_scalar(col("w3_s"), col("w3_s"), 1.0 / (9 * P), None, ALU.mult)
            v.tensor_scalar(col("q_b1"), col("q_b"), 1.0, None, ALU.add)
            v.tensor_scalar(col("q_nb"), col("q_b"), -1.0, None, ALU.mult)
            for conv in ("cpe1", "cpe2"):
                v.tensor_scalar(tap_weight(conv, (0, 0)), tap_weight(conv, (0, 0)), 1.0, None, ALU.add)
            link(v.reduce_sum(col("Dsum"), cols[:, at["l1_D"]:at["l1_D"] + 4], mybir.AxisListType.X))
            for conv in convs:
                for d, tap in zip(diag[conv], TAPS[CHAIN:]):
                    v.tensor_scalar(d[:, :], ident[:, :], tap_weight(conv, tap), None, ALU.mult)
            v.tensor_scalar(dwl1[:, :], same_half[:, :], col("l1taps", 5), None, ALU.mult)
            v.tensor_scalar(w_in[:, :], raw_in, col("n1_g"), None, ALU.mult)
            v.tensor_scalar(w_act[:, :], raw_act, col("n1_g"), None, ALU.mult)
            v.tensor_scalar(fc1[:, :], raw_fc1, col("n2_g"), None, ALU.mult)
            v.wait_ge(setup_pe, 1)
            v.tensor_copy(w_xc[:, :], psum[:, 0, 0:128])
            v.tensor_copy(w_z[:, :], psum[:, 0, 128:256])
            v.tensor_scalar(w_l1out[:, :], psum[:, 0, 256:384], col("l1_gb"), None, ALU.mult)
            v.tensor_copy(kbias[:, :], psum[:, 0, 384:512])
            for n in range(2):
                v.tensor_copy(w_dt[n][:, :], psum[:, 1, P * n:P * (n + 1)])
                v.tensor_copy(w_B[n][:, :], psum[:, 2, 2 * P * n:2 * P * n + P])
                v.tensor_copy(w_C[n][:, :], psum[:, 2, 2 * P * n + P:2 * P * (n + 1)])
            v.tensor_copy(col("xc_b"), psum[:, 3, 0:1])
            v.tensor_copy(col("z_b"), psum[:, 3, 1:2])
            v.tensor_tensor(col("in_o"), psum[:, 3, 2:3], col("in_b"), ALU.add)
            v.tensor_tensor(col("act_o"), psum[:, 3, 3:4], col("act_b"), ALU.add)
            v.tensor_tensor(cols[:, at["fc1_o"]:at["fc1_o"] + 4], psum[:, 3, 4:8], cols[:, at["fc1_b"]:at["fc1_b"] + 4], ALU.add)
            link(v.memset(R[0][:, :], 0.0))
            v.sem_inc(ready, 1)

            with v.Fori(0, B, 1) as i:
                def split(b, p):
                    xr = x_tile[p].rearrange("p (r w) -> p r w", w=S)
                    pairs = pair_sum[p].rearrange("p (r w) -> p r w", w=S // 2)
                    quads = quad_sum[p].rearrange("p (r w) -> p r w", w=S // 2)
                    wide = low_wide[p].rearrange("p (r w e) -> p r w e", w=S // 2, e=2)
                    wrows = low_wide[p].rearrange("p (r w) -> p r w", w=S)
                    v.wait_ge(x_in[p], landed(i, b, p))
                    v.tensor_tensor(pairs, xr[:, :, 0::2], xr[:, :, 1::2], ALU.add).then_inc(l0_steps, 1)
                    v.wait_ge(l0_steps, steps(i, b, 3, 1))
                    v.tensor_tensor(quads, pairs[:, 0::2, :], pairs[:, 1::2, :], ALU.add).then_inc(l0_steps, 1)
                    v.wait_ge(l0_steps, steps(i, b, 3, 2))
                    v.wait_ge(l0_mm, done(i, b - 2))
                    v.tensor_scalar(wide, quads.unsqueeze(3).broadcast_to((P, HALF, S // 2, 2)), 0.25, None, ALU.mult)\
                        .then_inc(l0_steps, 1)
                    v.wait_ge(l0_steps, steps(i, b, 3, 3))
                    v.tensor_tensor(high[p][:, 1:1 + ROWS, :].rearrange("p (r e) w -> p r e w", e=2),
                                    xr.rearrange("p (r e) w -> p r e w", e=2),
                                    wrows.unsqueeze(2).broadcast_to((P, HALF, 2, S)), ALU.subtract)
                    v.tensor_tensor(high[p][:, 0, :], xr[:, ROWS - 1, :], wrows[:, HALF - 1, :], ALU.subtract)\
                        .then_inc(l0_high, 1)

                def join(b, p):
                    lows = low_pos[p].rearrange("p (r w) -> p r w", w=S // 2)
                    v.wait_ge(l0_relu, done(i, b))
                    v.scalar_tensor_tensor(out=low_pos[p], in0=low_neg[p], scalar=col("nalpha"), in1=low_pos[p],
                                           op0=ALU.mult, op1=ALU.add).then_inc(l0_join, 1)
                    v.scalar_tensor_tensor(out=hs_pos[p], in0=hs_neg[p], scalar=col("nalpha"), in1=hs_pos[p],
                                           op0=ALU.mult, op1=ALU.add).then_inc(l0_join, 1)
                    v.wait_ge(l0_join, steps(i, b, 3, 1))
                    v.tensor_copy(out_low.rearrange("p (r w e) -> p r w e", w=S // 2, e=2),
                                  lows.unsqueeze(3).broadcast_to((P, HALF, S // 2, 2))).then_inc(l0_join, 1)
                    v.wait_ge(l0_join, steps(i, b, 3, 3))
                    v.tensor_tensor(prow(0, b).rearrange("p (r e) w -> p r e w", e=2),
                                    hs_pos[p].rearrange("p (r e w) -> p r e w", e=2, w=S),
                                    out_low.rearrange("p (r w) -> p r w", w=S).unsqueeze(2).broadcast_to((P, HALF, 2, S)),
                                    ALU.add).then_inc(l0_out, 1)

                def xc(b, p):
                    v.wait_ge(a_mm, done(i, b))
                    v.tensor_scalar(pad_rows(3, b, slice(0, CM)), rows_of(pair(3))[0:CM],
                                    col("xc_b", rows=slice(0, CM)), None, ALU.add).then_inc(a_xc, 1)

                pipelined(v, NB, [(4, xc), (0, split), (2, join)])

                def scan_tap_stage(n):
                    def stage(b, p):
                        sofar = by_row(tile(4 + p))
                        v.wait_ge(b_taps[n - 2], done(i, b))
                        if n == 4:
                            v.wait_ge(b_mm, done(i, b - 2))
                        v.scalar_tensor_tensor(out=by_row(tile(6 + p)) if n == 4 else sofar,
                                               in0=prow(3, b, *scan_tap(n)), scalar=col("l1taps", n), in1=sofar,
                                               op0=ALU.mult, op1=ALU.add).then_inc(b_taps[n - 1], 1)
                    return stage

                pipelined(v, NB, [(2, scan_tap_stage(n)) for n in (2, 3, 4)])

                for sweep in range(2):
                    c = c_sets[sweep]
                    edge = BLK - 1 if sweep == 0 else 0

                    def step_size(b, p):
                        v.wait_ge(c["log"], done(i, b))
                        v.wait_ge(c["relu"], done(i, b))
                        v.tensor_tensor(tile(p), tile(p), relu_tiles[:, BLK * p:BLK * (p + 1)], ALU.add).then_inc(c["step"], 1)

                    def input_term(b, p):
                        v.wait_ge(c["du"], done(i, b))
                        v.wait_ge(c["B"], done(i, b))
                        v.tensor_tensor(halves(tile(2 + p)), halves(tile(2 + p)), pair(4), ALU.mult).then_inc(c["bu"], 1)

                    def scan(b, p):
                        v.wait_ge(c["bu"], done(i, b))
                        v.wait_ge(c["decay"], done(i, b))
                        first = isinstance(b, int) and b == 0
                        start = col("zero") if first else tile(7 - p)[:, edge:edge + 1]
                        way = (lambda ap: ap) if sweep == 0 else (lambda ap: ap[:, ::-1])
                        v.tensor_tensor_scan(way(tile(6 + p)), way(tile(4 + p)), way(tile(2 + p)), initial=start,
                                             op0=ALU.mult, op1=ALU.add).then_inc(c["h"], 1)

                    def outputs(b, p):
                        v.wait_ge(c["h"], done(i, b))
                        v.wait_ge(c["C"], done(i, b))
                        y = flat(3, b) if sweep == 0 else tile(4 + p)
                        v.tensor_tensor(halves(y), halves(tile(6 + p)), pair(6), ALU.mult).then_inc(c["hc"], 1)

                    pipelined(v, NB, [(3, input_term), (3, scan), (3, outputs), (1, step_size)])

                def rows(b, p):
                    v.wait_ge(d_yc, done(i, b - 2))
                    v.scalar_tensor_tensor(out=tile(4 + p)[0:CM], in0=flat(2, b)[0:CM], scalar=col("Dsum", rows=slice(0, CM)),
                                           in1=flat(3, b)[0:CM], op0=ALU.mult, op1=ALU.add).then_inc(d_rows, 1)

                def normalise(b, p):
                    v.wait_ge(d_rstd, done(i, b))
                    v.wait_ge(d_gate, done(i, b - 2))
                    v.tensor_tensor(halves(tile(2 + p)), halves(tile(p)), pair(2 * p), ALU.mult).then_inc(d_norm, 1)

                def residual(b, p):
                    v.wait_ge(d_mm, done(i, b))
                    for s in range(2):
                        x = prow(0, b, rows=HALF, skip=HALF * s)
                        last = v.scalar_tensor_tensor(out=x, in0=pair(6)[:, s].rearrange("p (r w) -> p r w", w=S),
                                                      scalar=col("cv2_b"), in1=x, op0=ALU.add, op1=ALU.add)
                    last.then_inc(d_out, 1)

                all_done(v, i, c_sets[1]["y"])
                pipelined(v, NB, [(5, residual), (3, normalise), (0, rows)])

                def add_taps(b, p):
                    v.wait_ge(tap_done[-1], tapped(i, "cpe1", b))
                    v.wait_ge(e1["conv"], done(i, b))
                    v.tensor_tensor(prow(1, b).rearrange("p (a r) w -> p a r w", a=2), by_rows(chain_tile("cpe1", 2, p)),
                                    rows_of(pair(0)), ALU.add).then_inc(e1["t"], 1)

                def normalise(b, p):
                    v.wait_ge(e1["rstd"], done(i, b))
                    v.tensor_tensor(halves(flat(2, b)), halves(tile(2 + p)), pair(2 + 2 * p), ALU.mult)\
                        .then_inc(e1["tn"], 1)

                taps = [chain_tap(v, i, "cpe1", tap, 0, lambda p: chain_tile("cpe1", 2, p)) for tap in VECTOR_TAPS]
                pipelined(v, NB, [(5, normalise), (2, add_taps)] + [(1, tap) for tap in taps])

                def ti(b, p):
                    v.wait_ge(e2_mm, done(i, b))
                    v.tensor_scalar(prow(3, b).rearrange("p (a r) w -> p a r w", a=2), rows_of(pair(0)), col("in_o"),
                                    None, ALU.add).then_inc(e2_ti, 1)

                def add_taps(b, p):
                    v.wait_ge(tap_done[-1], tapped(i, "dwc", b))
                    v.wait_ge(e2_conv, done(i, b))
                    v.wait_ge(e2_v, done(i, b - 2))
                    v.tensor_tensor(halves(tile(2 + p)), halves(chain_tile("dwc", 2, p)), pair(4 + 2 * p), ALU.add)\
                        .then_inc(e2_sum, 1)

                taps = [chain_tap(v, i, "dwc", tap, 3, lambda p: chain_tile("dwc", 2, p)) for tap in VECTOR_TAPS]
                pipelined(v, NB, [(1, ti), (4, taps[0]), (5, add_taps), (4, taps[1]), (4, taps[2]), (4, taps[3])])

                def key_in(b, p):
                    v.wait_ge(f1_mm, done(i, b))
                    v.wait_ge(f1_kc, done(i, b - 2))
                    v.wait_ge(f1_ksum, done(i, b - 2))
                    v.wait_ge(f1_ks, done(i, b - 2))
                    v.tensor_tensor(by_tile(tile(p)), token_psum(p)[:, :, 0:P],
                                    kbias[:, :].unsqueeze(1).broadcast_to((P, NT, P)), ALU.add).then_inc(f1_bias, 1)
                    v.wait_ge(f1_bias, done(i, b))
                    if is_first(b):
                        v.wait_ge(e2_v, done(i, NB - 1))
                    v.tensor_scalar(tile(2 + p), tile(p), 0.0, None, ALU.min).then_inc(f1_min, 1)

                def key_phi(b, p):
                    v.wait_ge(f1_exp, done(i, b))
                    v.scalar_tensor_tensor(out=tile(p), in0=tile(p), scalar=1.0, in1=tile(2 + p), op0=ALU.add,
                                           op1=ALU.max).then_inc(f1_k, 1)

                def key_turned(b, p):
                    v.wait_ge(f1_k, done(i, b))
                    v.wait_ge(f1_tab[p], landed(i, b, p))
                    v.wait_ge(f1_kv, done(i, b - 2))
                    for which, given in enumerate((f1_kc, f1_ks)):
                        v.tensor_tensor(by_pairs(kcs(p)[:, :, P * which:P * (which + 1)]), by_pairs(by_tile(tile(p))),
                                        tok_table(p, which), ALU.mult).then_inc(given, 1)

                pipelined(v, NB, [(3, key_phi), (2, key_in), (3, key_turned)])

                all_done(v, i, f1_kv)
                v.tensor_copy(region_tile(3, 8)[:, 0:2 * P], psum[:, 6, 0:2 * P]).then_inc(kv_vec, 1)
                v.wait_ge(kv_pe, i * 3 + 1)
                v.tensor_copy(region_tile(3, 9)[:, 0:2 * P], psum[:, 7, 0:2 * P])
                v.tensor_scalar(kmean[:, :], headmask[:, :], psum[:, 6, 300:301], 1.0 / N, ALU.mult, ALU.mult)\
                    .then_inc(kv_vec, 1)
                v.wait_ge(kv_pe, i * 3 + 2)
                v.scalar_tensor_tensor(out=kv[:, :], in0=psum[:, 0, 0:P], scalar=1.0 / N, in1=headmask[:, :],
                                       op0=ALU.mult, op1=ALU.mult).then_inc(kv_vec, 1)
                v.wait_ge(kv_pe, i * 3 + 3)
                v.tensor_copy(kv_rot[:, :], psum[:, 1, 0:P]).then_inc(kv_vec, 1)

                def add_taps(b, p):
                    v.wait_ge(tap_done[-1], tapped(i, "lepe", b))
                    v.wait_ge(f2_conv, done(i, b))
                    v.wait_ge(f2_sum, done(i, b - 2))
                    v.tensor_tensor(halves(tile(6 + p)), halves(tile(4 + p)), pair(6), ALU.add).then_inc(f2_lepe, 1)

                def query_phi(b, p):
                    v.wait_ge(f2_exp, done(i, b))
                    v.wait_ge(f2_den, done(i, b - 2))
                    v.wait_ge(f2_qs, done(i, b - 2))
                    v.scalar_tensor_tensor(out=halves(tile(p)), in0=pair(0), scalar=col("q_b1"),
                                           in1=halves(region_tile(3, 8 + p)), op0=ALU.add, op1=ALU.max).then_inc(f2_phi, 1)

                def attention(b, p):
                    v.wait_ge(f2_num, done(i, b))
                    v.wait_ge(f2_z, done(i, b))
                    v.wait_ge(f2_out, done(i, b - 2))
                    v.tensor_tensor(halves(tile(2 + p)), halves(region_tile(3, 10 + p)), pair(4), ALU.mult)\
                        .then_inc(f2_nz, 1)

                def residual2(b, p):
                    v.wait_ge(f2_out, done(i, b))
                    for s in range(2):
                        x = prow(1, b, rows=HALF, skip=HALF * s)
                        last = v.scalar_tensor_tensor(out=x, in0=pair(2)[:, s].rearrange("p (r w) -> p r w", w=S),
                                                      scalar=col("out_b"), in1=x, op0=ALU.add, op1=ALU.add)
                    last.then_inc(f2_t2, 1)

                taps = [chain_tap(v, i, "lepe", tap, 0, lambda p: tile(4 + p)) for tap in TERM_TAPS + VECTOR_TAPS]
                pipelined(v, NB, [(2, add_taps), (1, taps[0]), (1, query_phi), (1, taps[1]), (1, taps[2]), (1, taps[3]),
                                  (4, residual2), (1, taps[4]), (2, attention), (1, taps[5])])

                def tap_7(b, p):
                    acc = by_row(chain_tile("cpe2", 2, p))
                    v.wait_ge(tap_done[-1], tapped(i, "cpe2", b))
                    v.scalar_tensor_tensor(out=acc, in0=prow(1, b, *TAPS[7]), scalar=tap_weight("cpe2", TAPS[7]), in1=acc,
                                           op0=ALU.mult, op1=ALU.add).then_inc(g_tap7, 1)

                def tap_8(b, p):
                    v.wait_ge(g_tap7, done(i, b))
                    v.scalar_tensor_tensor(out=by_row(flat(3, b)), in0=prow(1, b, *TAPS[8]),
                                           scalar=tap_weight("cpe2", TAPS[8]), in1=by_row(chain_tile("cpe2", 2, p)),
                                           op0=ALU.mult, op1=ALU.add).then_inc(g_t, 1)

                def g_normalise(b, p):
                    v.wait_ge(g_rstd, done(i, b))
                    v.tensor_tensor(halves(flat(2, b)), halves(tile(2 + p)), pair(2), ALU.mult).then_inc(g_tn, 1)

                def x3(b, p):
                    v.wait_ge(g_fc2, done(i, b))
                    v.scalar_tensor_tensor(out=halves(flat(3, b)), in0=pair(4), scalar=col("fc2_b"),
                                           in1=halves(flat(3, b)), op0=ALU.add, op1=ALU.add).then_inc(g_x3, 1)

                taps = [chain_tap(v, i, "cpe2", tap, 1, lambda p: chain_tile("cpe2", 2, p)) for tap in VECTOR_TAPS]
                pipelined(v, NB, [(1, taps[0]), (1, taps[1]), (5, x3), (1, taps[2]), (1, taps[3]), (1, tap_7), (1, tap_8),
                                  (3, g_normalise)])


def constants(S):
    f = np.float32
    c, d = np.arange(P)[:, None], np.arange(P)[None, :]
    eye = (c == d).astype(f)
    same_half = (c % CM == d % CM).astype(f)
    cen64 = same_half - f(1 / CM)
    rot = np.zeros((P, P), f)
    rot[0::2, 1::2][np.arange(P // 2), np.arange(P // 2)] = -1
    rot[1::2, 0::2][np.arange(P // 2), np.arange(P // 2)] = 1
    half = np.zeros((2, P), f)
    half[0, :CM], half[1, CM:] = 1, 1
    out = {"c_ident": eye, "c_cen128": eye - f(1 / P), "c_avg128": np.full((P, P), 1 / P, f),
           "c_headmask": (c // (P // HEADS) == d // (P // HEADS)).astype(f), "c_rot": rot, "c_rotT": rot.T.copy(),
           "c_cen64": cen64, "c_e2": same_half, "c_half": half}
    k = P // 4
    theta = f(1) / (f(10000.0) ** (np.arange(k, dtype=f) / f(k))).astype(f)
    at = (np.arange(S, dtype=f)[:, None] * theta).astype(f)
    ang = np.concatenate([np.broadcast_to(at[:, None, :], (S, S, k)), np.broadcast_to(at[None, :, :], (S, S, k))], -1)
    nb, blk = S // ROWS, ROWS * S
    ang = ang.reshape(nb, blk, 2 * k)
    cs = np.stack([np.cos(ang), np.sin(ang)]).astype(f)
    tok = cs.reshape(2, nb, blk // P, P, 2 * k).transpose(1, 3, 0, 2, 4).reshape(nb, P, blk)
    ch = np.repeat(cs, 2, axis=3).transpose(1, 3, 0, 2).reshape(nb, P, 2 * blk)
    out["tab_tok"], out["tab_ch"] = np.ascontiguousarray(tok), np.ascontiguousarray(ch)
    return out


def layout(x):
    g = {k: np.asarray(v) for k, v in x.items()}
    l0 = {k[8:]: v for k, v in g.items() if k.startswith("L0_conv_")}
    l1 = {k[8:]: v for k, v in g.items() if k.startswith("L1_conv_")}
    l2 = {k[8:]: v for k, v in g.items() if k.startswith("L2_conv_")}
    w3 = g["L3_conv_weight"]
    a = constants(g["x"].shape[-1])
    a["x"] = g["x"]
    a["ph_aT"], a["ph_bT"] = l0["phase_w"][:P, :P].T, l0["phase_w"][:P, P:].T
    a["magT"] = l0["mag_w"].T
    a["inprojT"], a["cv1_w"], a["out_proj"] = l1["in_proj_w"].T, l1["cv1_w"], l1["out_proj_w"]
    a["cv2T"], a["x_proj"], a["dt_wT"] = l1["cv2_w"].T, l1["x_proj_w"], l1["dt_w"].transpose(0, 2, 1)
    for name in ("inproj_w", "actproj_w", "fc1_w", "fc2_w", "qk_w", "outproj_w"):
        a[name] = l2[name]
    a["kb_row"] = l2["qk_b"][None, P:]
    a["w3_nat"] = w3.reshape(P, 9 * P)
    a["w3_T"] = w3.transpose(1, 2, 3, 0).reshape(P, 9 * P)

    def twice(v):
        return np.concatenate([v, v])

    A, Ds, cw = l1["A_logs"].reshape(4, CM), l1["Ds"].reshape(4, CM), l1["conv_w"].reshape(CM, 9)
    columns = {
        "mag_b": l0["mag_b"], "mag_gamma": l0["mag_gamma"], "mag_beta": l0["mag_beta"], "mag_mean": l0["mag_mean"],
        "mag_var": l0["mag_var"], "ph_b": l0["phase_b"][:P], "ph_gamma": l0["phase_gamma"][:P],
        "ph_beta": l0["phase_beta"][:P], "ph_mean": l0["phase_mean"][:P], "ph_var": l0["phase_var"][:P],
        "alpha": np.repeat(l0["alpha"], P), "l1_dtb0": l1["dt_b"][:2].ravel(), "l1_dtb1": l1["dt_b"][2:].ravel(),
        "l1_A0": A[:2].ravel(), "l1_A1": A[2:].ravel(), "l1_gb": np.concatenate([l1["ln_g"], l1["ln_b"]]),
        "l1_scale": twice(l1["scale_w"].ravel()), "l1_cb": twice(l1["conv_b"]), "l1_cv1b": twice(l1["cv1_b"]),
        "cv2_b": l1["cv2_b"], "cpe1_b": l2["cpe1_b"], "n1_g": l2["n1_g"], "n1_b": l2["n1_b"], "in_b": l2["inproj_b"],
        "act_b": l2["actproj_b"], "dwc_b": l2["dwc_b"], "q_b": l2["qk_b"][:P], "lepe_b": l2["lepe_b"],
        "out_b": l2["outproj_b"], "cpe2_b": l2["cpe2_b"], "n2_g": l2["n2_g"], "n2_b": l2["n2_b"], "fc2_b": l2["fc2_b"],
        "fc1_b": l2["fc1_b"].reshape(4, P).T,
        "taps": np.concatenate([l2[c + "_w"].reshape(P, 9) for c in ("cpe1", "dwc", "lepe", "cpe2")], axis=1),
        "l1taps": np.concatenate([np.concatenate([cw[:, 0:3], cw[:, 3:6]]),
                                  np.concatenate([cw[:, 6:9], np.zeros((CM, 3), cw.dtype)])], axis=1),
        "l1_D": twice(Ds.T),
    }
    a["cols"] = np.concatenate([columns[n].reshape(P, -1) for n in HOST_COLS], axis=1)
    return {k: np.ascontiguousarray(v) for k, v in a.items()}


def kernel(**inputs):
    import concourse.bacc as bacc
    from concourse.bass_utils import run_bass_kernel_spmd

    arrays = layout(inputs)
    nc = bacc.Bacc("TRN2", target_bir_lowering=False, num_devices=1)
    aps = {k: nc.dram_tensor("in_" + k, v.shape, mybir.dt.from_np(v.dtype), kind="ExternalInput").ap()
           for k, v in arrays.items()}
    out = nc.dram_tensor("out", arrays["x"].shape, F32, kind="ExternalOutput").ap()
    build(nc, aps, out)
    got = run_bass_kernel_spmd(nc, [{"in_" + k: v for k, v in arrays.items()}], core_ids=[0])
    return got.results[0]["out"]
```
